# Optimizing a Trainium2 kernel written in Bass

```python
import numpy as np
import jax
import jax.numpy as jnp

def _softmax(x, axis=-1):
    return jax.nn.softmax(x, axis=axis)

def _gelu(x):
    return jax.nn.gelu(x, approximate=True)

def _silu(x):
    return jax.nn.silu(x)

def _sigmoid(x):
    return jax.nn.sigmoid(x)

def _layernorm(x, axis=-1, eps=1e-05):
    m = jnp.mean(x, axis=axis, keepdims=True)
    v = jnp.var(x, axis=axis, keepdims=True)
    return (x - m) / jnp.sqrt(v + eps)

def _scatter_add(tgt, idx, src, axis=0):
    return tgt.at[idx].add(src)

def _segment_sum(src, seg, n):
    return jax.ops.segment_sum(src, seg, n)
kernel_name = 'mk_adj_preln_d2_adj_r2_51fefb'

def setup_inputs(seed: int=0):
    np.random.seed(seed)
    _w = jnp.asarray

    def _rec_inputs():
        import jax
        import jax.numpy as jnp
        _gk = jax.random.key(seed)
        x = -0.0001538 + 1 * jax.random.normal(jax.random.fold_in(_gk, 1), (128, 128, 384), jnp.float32)
        _a = jax.random.bernoulli(jax.random.fold_in(_gk, 2), 0.0625, (128, 128, 128))
        _a = jnp.logical_or(_a, jnp.swapaxes(_a, -1, -2))
        _a = jnp.logical_or(_a, jnp.eye(128, dtype=bool))
        adj = _a
        return (x, adj)
    x, adj = _rec_inputs()

    def _L0_gnn_setup():
        import jax, jax.numpy as jnp
        import numpy as np
        B, S, H = (4, 1024, 384)
        NUM_HEADS = 6
        HEAD_SIZE = H // NUM_HEADS
        NEG = -9000000000000000.0

        def _heads(x):
            b, s, _ = x.shape
            return x.reshape(b, s, NUM_HEADS, HEAD_SIZE).transpose(0, 2, 1, 3)
        key = jax.random.key(seed)
        ks = jax.random.split(key, 10)
        seq_inputs = jax.random.normal(ks[0], (B, S, H), dtype=jnp.float32)
        gm = jax.random.randint(ks[1], (B, S, S), 0, 2) > 0
        graph_mask = gm | jnp.eye(S, dtype=bool)[None]
        sc = 1.0 / np.sqrt(H)
        Wq = jax.random.normal(ks[2], (H, H), dtype=jnp.float32) * sc
        bq = jnp.zeros((H,), dtype=jnp.float32)
        Wk = jax.random.normal(ks[3], (H, H), dtype=jnp.float32) * sc
        bk = jnp.zeros((H,), dtype=jnp.float32)
        Wv = jax.random.normal(ks[4], (H, H), dtype=jnp.float32) * sc
        bv = jnp.zeros((H,), dtype=jnp.float32)
        Wf = jax.random.normal(ks[5], (H, H), dtype=jnp.float32) * sc
        bf = jnp.zeros((H,), dtype=jnp.float32)
        return {'seq_inputs': seq_inputs, 'Wq': Wq, 'bq': bq, 'Wk': Wk, 'bk': bk, 'Wv': Wv, 'bv': bv, 'Wf': Wf, 'bf': bf, 'graph_mask': graph_mask}
    _L0_gnn_all = _L0_gnn_setup()
    _L0_gnn_in = {k: v for k, v in _L0_gnn_all.items() if k in ('Wq', 'bq', 'Wk', 'bk', 'Wv', 'bv', 'Wf', 'bf')}
    del _L0_gnn_all

    def _L1_gnn_setup():
        import jax, jax.numpy as jnp
        import numpy as np
        B, S, H = (4, 1024, 384)
        NUM_HEADS = 6
        HEAD_SIZE = H // NUM_HEADS
        NEG = -9000000000000000.0

        def _heads(x):
            b, s, _ = x.shape
            return x.reshape(b, s, NUM_HEADS, HEAD_SIZE).transpose(0, 2, 1, 3)
        key = jax.random.key(seed)
        ks = jax.random.split(key, 10)
        seq_inputs = jax.random.normal(ks[0], (B, S, H), dtype=jnp.float32)
        gm = jax.random.randint(ks[1], (B, S, S), 0, 2) > 0
        graph_mask = gm | jnp.eye(S, dtype=bool)[None]
        sc = 1.0 / np.sqrt(H)
        Wq = jax.random.normal(ks[2], (H, H), dtype=jnp.float32) * sc
        bq = jnp.zeros((H,), dtype=jnp.float32)
        Wk = jax.random.normal(ks[3], (H, H), dtype=jnp.float32) * sc
        bk = jnp.zeros((H,), dtype=jnp.float32)
        Wv = jax.random.normal(ks[4], (H, H), dtype=jnp.float32) * sc
        bv = jnp.zeros((H,), dtype=jnp.float32)
        Wf = jax.random.normal(ks[5], (H, H), dtype=jnp.float32) * sc
        bf = jnp.zeros((H,), dtype=jnp.float32)
        return {'seq_inputs': seq_inputs, 'Wq': Wq, 'bq': bq, 'Wk': Wk, 'bk': bk, 'Wv': Wv, 'bv': bv, 'Wf': Wf, 'bf': bf, 'graph_mask': graph_mask}
    _L1_gnn_all = _L1_gnn_setup()
    _L1_gnn_in = {k: v for k, v in _L1_gnn_all.items() if k in ('Wq', 'bq', 'Wk', 'bk', 'Wv', 'bv', 'Wf', 'bf')}
    del _L1_gnn_all
    return {'x': x, 'adj': adj, 'L0_gnn_Wq': _L0_gnn_in['Wq'], 'L0_gnn_bq': _L0_gnn_in['bq'], 'L0_gnn_Wk': _L0_gnn_in['Wk'], 'L0_gnn_bk': _L0_gnn_in['bk'], 'L0_gnn_Wv': _L0_gnn_in['Wv'], 'L0_gnn_bv': _L0_gnn_in['bv'], 'L0_gnn_Wf': _L0_gnn_in['Wf'], 'L0_gnn_bf': _L0_gnn_in['bf'], 'L1_gnn_Wq': _L1_gnn_in['Wq'], 'L1_gnn_bq': _L1_gnn_in['bq'], 'L1_gnn_Wk': _L1_gnn_in['Wk'], 'L1_gnn_bk': _L1_gnn_in['bk'], 'L1_gnn_Wv': _L1_gnn_in['Wv'], 'L1_gnn_bv': _L1_gnn_in['bv'], 'L1_gnn_Wf': _L1_gnn_in['Wf'], 'L1_gnn_bf': _L1_gnn_in['bf']}

def reference(x, adj, L0_gnn_Wq, L0_gnn_bq, L0_gnn_Wk, L0_gnn_bk, L0_gnn_Wv, L0_gnn_bv, L0_gnn_Wf, L0_gnn_bf, L1_gnn_Wq, L1_gnn_bq, L1_gnn_Wk, L1_gnn_bk, L1_gnn_Wv, L1_gnn_bv, L1_gnn_Wf, L1_gnn_bf):
    import jax
    import jax.numpy as jnp

    def _L0_gnn_ref(seq_inputs, Wq, bq, Wk, bk, Wv, bv, Wf, bf, graph_mask):
        import jax, jax.numpy as jnp
        import numpy as np
        B, S, H = (4, 1024, 384)
        NUM_HEADS = 6
        HEAD_SIZE = H // NUM_HEADS
        NEG = -9000000000000000.0

        def _heads(x):
            b, s, _ = x.shape
            return x.reshape(b, s, NUM_HEADS, HEAD_SIZE).transpose(0, 2, 1, 3)
        q = _heads(seq_inputs @ Wq + bq)
        k = _heads(seq_inputs @ Wk + bk)
        v = _heads(seq_inputs @ Wv + bv)
        scores = jnp.einsum('bhqd,bhkd->bhqk', q, k) / np.sqrt(HEAD_SIZE)
        bias = jnp.where(graph_mask, 0.0, NEG)[:, None]
        probs = jax.nn.softmax(scores + bias, axis=-1)
        ctx = jnp.einsum('bhqk,bhkd->bhqd', probs, v)
        ctx = ctx.transpose(0, 2, 1, 3).reshape(seq_inputs.shape[0], seq_inputs.shape[1], H)
        return ctx @ Wf + bf

    def _L1_gnn_ref(seq_inputs, Wq, bq, Wk, bk, Wv, bv, Wf, bf, graph_mask):
        import jax, jax.numpy as jnp
        import numpy as np
        B, S, H = (4, 1024, 384)
        NUM_HEADS = 6
        HEAD_SIZE = H // NUM_HEADS
        NEG = -9000000000000000.0

        def _heads(x):
            b, s, _ = x.shape
            return x.reshape(b, s, NUM_HEADS, HEAD_SIZE).transpose(0, 2, 1, 3)
        q = _heads(seq_inputs @ Wq + bq)
        k = _heads(seq_inputs @ Wk + bk)
        v = _heads(seq_inputs @ Wv + bv)
        scores = jnp.einsum('bhqd,bhkd->bhqk', q, k) / np.sqrt(HEAD_SIZE)
        bias = jnp.where(graph_mask, 0.0, NEG)[:, None]
        probs = jax.nn.softmax(scores + bias, axis=-1)
        ctx = jnp.einsum('bhqk,bhkd->bhqd', probs, v)
        ctx = ctx.transpose(0, 2, 1, 3).reshape(seq_inputs.shape[0], seq_inputs.shape[1], H)
        return ctx @ Wf + bf
    h = jnp.maximum(_layernorm(x, axis=-1), 0.0)
    x = x + _L0_gnn_ref(h, L0_gnn_Wq, L0_gnn_bq, L0_gnn_Wk, L0_gnn_bk, L0_gnn_Wv, L0_gnn_bv, L0_gnn_Wf, L0_gnn_bf, adj)
    h = jnp.maximum(_layernorm(x, axis=-1), 0.0)
    x = x + _L1_gnn_ref(h, L1_gnn_Wq, L1_gnn_bq, L1_gnn_Wk, L1_gnn_bk, L1_gnn_Wv, L1_gnn_bv, L1_gnn_Wf, L1_gnn_bf, adj)
    return x

_drawn_inputs = setup_inputs


def setup_inputs(seed=0):
    import zlib

    import numpy as np

    out = dict(_drawn_inputs(seed))
    spreads = {'L0_gnn_bq': (0.0, 0.8),
     'L0_gnn_bk': (0.0, 0.8),
     'L0_gnn_bv': (0.0, 0.1),
     'L0_gnn_bf': (0.0, 0.1),
     'L1_gnn_bq': (0.0, 0.8),
     'L1_gnn_bk': (0.0, 0.8),
     'L1_gnn_bv': (0.0, 0.1),
     'L1_gnn_bf': (0.0, 0.1)}
    factors = {}
    for name, (base, spread) in spreads.items():
        noise = np.random.default_rng([zlib.crc32(name.encode()), seed]).standard_normal(out[name].shape)
        drawn = base * np.exp(spread * noise) if base else spread * noise
        out[name] = jnp.asarray(drawn.astype(out[name].dtype))
    for name, factor in factors.items():
        out[name] = (out[name] * factor).astype(out[name].dtype)
    return out
```

```python
from contextlib import ExitStack

import numpy as np

import concourse.bass as bass
from concourse import mybir

F32 = mybir.dt.float32
F16 = mybir.dt.float16
U8 = mybir.dt.uint8
I32 = mybir.dt.int32
ALU = mybir.AluOpType
ACT = mybir.ActivationFunctionType
AX_X = mybir.AxisListType.X

P = 128
EPS = 1e-5
NEG = 9000000000000000.0
LAYERS = 2


def build(nc, x, adj, layers, out):
    GRAPHS, NODES, H = x.shape
    HEADS = 6
    DH = H // HEADS
    KT = H // P
    PER = 4
    TOK = PER * NODES
    GROUPS = GRAPHS // PER
    VW = DH + 2
    PAIRS = HEADS // 2
    assert NODES == P and GROUPS % 2 == 0

    HS = 4.0
    PROJ_TOP = 2.0 ** 12
    OUT_TOP = 2.0 ** 8
    LEAST = 2.0 ** -20

    FIRST, LAST = -2, 2 * GROUPS + 2
    HOLES = (1, 2 * GROUPS)
    LOOP_AT = 4
    BODY = 4
    CONSTS = 11
    ROUNDS = (2 * GROUPS - 2 - LOOP_AT) // BODY - 0
    JOBS = PER + 2 * KT
    CHUNKS_OF_STEP = ((0,), (1, 2), (3,), (4, 5))

    def exists(t):
        return 0 <= t <= LAST - 1 and t not in HOLES

    def unit_no(t):
        return min(t, LAST) - sum(h < t for h in HOLES)

    def layer_of(t):
        return t % 2

    def group_of(t):
        return t // 2 if t % 2 == 0 else (t - 3) // 2

    def job_of_v(i):
        return i + sum(len(c) for c in CHUNKS_OF_STEP[:i])

    def job_of_chunk(c):
        i = next(j for j, cs in enumerate(CHUNKS_OF_STEP) if c in cs)
        return job_of_v(i) + 1 + CHUNKS_OF_STEP[i].index(c)

    def unit_count(t, m, each=1, plus=0):
        return each * unit_no(t) + plus + (m * (each * BODY) if m is not None else 0)

    def group_count(t, m, each=1, plus=0):
        return each * group_of(t) + plus + (m * (each * BODY // 2) if m is not None else 0)

    def round_count(t, m, group, each=16):
        no = group_of(t) if group else unit_no(t)
        per = BODY // 4 if group else BODY // 2
        return each * (no // 2 + 1) + (m * (each * per) if m is not None else 0)

    def wait(eng, sem, value):
        if isinstance(value, int) and value <= 0:
            return
        eng.wait_ge(sem, value)

    def wait_apart(eng, count, sem, value):
        if isinstance(value, int):
            wait(eng, sem, value)
            return
        eng.reg_mov(count, value)
        eng.wait_ge(consts_set, CONSTS)
        eng.wait_ge(sem, count)

    def lag_of(t, i):
        return (t, i - 1) if i else (t - 1, PER - 1)

    def over_slots(eng, slot):
        for t in range(FIRST, LOOP_AT):
            slot(t, None)
        with eng.Fori(0, ROUNDS) as m:
            for t in range(LOOP_AT, LOOP_AT + BODY):
                slot(t, m)
        for t in range(LOOP_AT + BODY * ROUNDS, LAST + 1):
            slot(t, None)

    with ExitStack() as ctx:
        def sb(name, shape, dt):
            return ctx.enter_context(nc.sbuf_tensor(name, shape, dt))

        def bank(name):
            return ctx.enter_context(nc.psum_tensor(name, [P, 512], F32))

        def sem(name):
            return ctx.enter_context(nc.semaphore(name))

        NAMES = ("q", "k", "v", "f")
        w_raw = [sb(f"w_raw_{n}", [P, KT, H], F32) for n in NAMES]
        w_hi = [[sb(f"w{n}_hi{l}", [P, KT, H], F16) for n in NAMES] for l in range(LAYERS)]
        w_lo = [[sb(f"w{n}_lo{l}", [P, KT, H], F16) for n in NAMES] for l in range(LAYERS)]
        qk_bias_raw = sb("qk_bias_raw", [P, 2, KT], F32)
        v_bias_raw = sb("v_bias_raw", [P, KT], F32)
        f_bias_raw = sb("f_bias_raw", [1, H], F32)
        qk_bias = [sb(f"qk_bias{l}", [P, 2, KT], F32) for l in range(LAYERS)]
        out_bias = [sb(f"out_bias{l}", [P, H], F32) for l in range(LAYERS)]
        v_bias_wide = sb("v_bias_wide", [P, KT, P], F32)
        ones = sb("ones", [P, P], F32)
        ident = sb("ident", [P, P], F32)
        minus_half = sb("minus_half", [P, 1], F32)
        largest = sb("largest", [P, 6], F32)
        largest_all = sb("largest_all", [P, 6], F32)
        bound = sb("bound", [P, 4], F32)
        power = sb("power", [P, 4], F32)
        inverse = sb("inverse", [P, 4], F32)
        w_scale = sb("w_scale", [P, 4], F32)
        b_scale = sb("b_scale", [P, 2], F32)
        both = sb("both", [P, 2], F32)
        exp_scale = [sb(f"exp_scale{l}", [P, 1], F32) for l in range(LAYERS)]
        out_scale = [sb(f"out_scale{l}", [P, 1], F32) for l in range(LAYERS)]
        exp_inverse = sb("exp_inverse", [P, 1], F32)
        mask_scale = [sb(f"mask_scale{l}", [P, 1], F32) for l in range(LAYERS)]
        mask_shift = [sb(f"mask_shift{l}", [P, 1], F32) for l in range(LAYERS)]

        x0 = [sb(f"x0_{g}", [P, PER, H], F32) for g in range(2)]
        x1 = [sb(f"x1_{g}", [P, PER, H], F32) for g in range(2)]
        x2 = sb("x2", [P, PER, H], F32)
        adj_u8 = [sb(f"adj_u8_{b}", [P, PER, NODES], U8) for b in range(2)]
        mask = [sb(f"mask{b}", [P, PER, NODES], F32) for b in range(2)]
        stats = sb("stats", [P, 6], F32)
        mean_var = sb("mean_var", [P, 2], F32)
        var_eps = sb("var_eps", [P, 1], F32)
        rstd = sb("rstd", [P, 1], F32)
        shift = sb("shift", [P, 1], F32)
        h = sb("h", [P, H], F32)
        ht_hi = [sb(f"ht_hi{b}", [P, KT, TOK], F16) for b in range(2)]
        ht_lo = [sb(f"ht_lo{b}", [P, KT, TOK], F16) for b in range(2)]
        qk_hi = [sb(f"qk_hi{b}", [P, 2 * KT, TOK], F16) for b in range(2)]
        qk_lo = [sb(f"qk_lo{b}", [P, 2 * KT, TOK], F16) for b in range(2)]
        v_hi = [sb(f"v_hi{b}", [P, PER, HEADS, VW], F16) for b in range(2)]
        v_lo = [sb(f"v_lo{b}", [P, PER, HEADS, VW], F16) for b in range(2)]
        probs = sb("probs", [P, HEADS, NODES], F32)
        row_max = sb("row_max", [P, HEADS], F32)
        pt_hi = sb("pt_hi", [P, HEADS, NODES], F16)
        pt_lo = sb("pt_lo", [P, HEADS, NODES], F16)
        row_rcp = sb("row_rcp", [P, HEADS], F32)
        ctx_n = sb("ctx_n", [P, HEADS, DH], F32)
        ct_hi = sb("ct_hi", [P, KT, NODES], F16)
        ct_lo = sb("ct_lo", [P, KT, NODES], F16)

        ps_scores = [bank("ps_scores0"), bank("ps_scores1")]
        ps_pt = [bank("ps_pt0"), bank("ps_pt1")]
        ps_turn = bank("ps_turn")
        ps_out = bank("ps_out")
        ps_proj = [bank("ps_proj0"), bank("ps_proj1")]

        x_loaded = [sem("x_loaded0"), sem("x_loaded1")]
        adj_loaded = [sem("adj_loaded0"), sem("adj_loaded1")]
        w_loaded = [sem(f"w_loaded_{n}") for n in NAMES]
        b_loaded = sem("b_loaded")
        consts_set = sem("consts_set")
        ident_set = sem("ident_set")
        setup_chain = sem("setup_chain")
        largest_found = sem("largest_found")
        largest_shared = sem("largest_shared")
        scales_set = sem("scales_set")
        w_hi_set = sem("w_hi_set")
        weights_set = sem("weights_set")
        v_bias_spread = sem("v_bias_spread")
        out_bias_summed = sem("out_bias_summed")
        out_bias_set = sem("out_bias_set")
        mask_set = sem("mask_set")
        stats_found = sem("stats_found")
        mean_found = sem("mean_found")
        var_ready = sem("var_ready")
        rstd_ready = sem("rstd_ready")
        norm_ready = sem("norm_ready")
        h_ready = sem("h_ready")
        res_ready = sem("res_ready")
        ht_turned = sem("ht_turned")
        ht_hi_set = sem("ht_hi_set")
        ht_set = sem("ht_set")
        projected = sem("projected")
        proj_hi_set = sem("proj_hi_set")
        proj_set = sem("proj_set")
        scored = sem("scored")
        masked = sem("masked")
        shifted = sem("shifted")
        exp_done = sem("exp_done")
        pt_turned = sem("pt_turned")
        pt_hi_set = sem("pt_hi_set")
        pt_set = sem("pt_set")
        ctx_summed = sem("ctx_summed")
        rcp_ready = sem("rcp_ready")
        ctx_ready = sem("ctx_ready")
        ct_turned = sem("ct_turned")
        ct_hi_set = sem("ct_hi_set")
        ct_set = sem("ct_set")
        out_summed = sem("out_summed")
        out_added = sem("out_added")
        stored = [sem(f"stored{i}") for i in range(PER)]

        def head_of(s):
            return 2 * (s % PAIRS) + s // PAIRS

        block = ctx.enter_context(nc.Block())

        @block.sync
        def _(sp):
            count = sp.alloc_register("count")

            def load_x(t, m):
                first = sp.snap(group_count(t, m, PER)) if m is not None else group_count(t, m, PER)
                if group_of(t) >= 2:
                    wait_apart(sp, count, out_added, unit_count(t - 4, m, PER, PER))
                sp.dma_start(x0[group_of(t) % 2][:, :, :],
                             x[bass.ds(first, PER), :, :].rearrange("b n d -> n b d")
                             ).then_inc(x_loaded[group_of(t) % 2], 16)

            def load_adj(t, m):
                first = sp.snap(group_count(t, m, PER)) if m is not None else group_count(t, m, PER)
                if unit_no(t) >= 2:
                    wait_apart(sp, count, mask_set, unit_count(t, m, 1, -1))
                sp.dma_start(adj_u8[unit_no(t) % 2][:, :, :],
                             adj[bass.ds(first, PER), :, :].rearrange("b q k -> q b k")
                             ).then_inc(adj_loaded[unit_no(t) % 2], 16)

            def load_weights(l):
                if l:
                    sp.wait_ge(weights_set, 4)
                    sp.wait_ge(out_bias_summed, 1)
                wts = layers[l]
                with nc.allow_non_contiguous_dma(reason="3 x 384 bias values, once a layer"):
                    for j, b in enumerate(("bq", "bk")):
                        sp.dma_start(qk_bias_raw[:, j, :], wts[b].rearrange("(c p) -> p c", p=P)).then_inc(b_loaded, 16)
                    sp.dma_start(v_bias_raw[:, :], wts["bv"].rearrange("(c p) -> p c", p=P)).then_inc(b_loaded, 16)
                sp.dma_start(f_bias_raw[:, :], wts["bf"].rearrange("(a n) -> a n", a=1)).then_inc(b_loaded, 16)
                for j, w in enumerate(("Wq", "Wk", "Wv", "Wf")):
                    sp.dma_start(w_raw[j][:, :, :], wts[w].rearrange("(c p) n -> p c n", p=P)).then_inc(w_loaded[j], 16)

            def slot(t, m):
                if t == 0:
                    load_weights(1)
                for i in range(PER):
                    lt, li = lag_of(t, i)
                    if i == 0 and exists(t + 2):
                        load_adj(t + 2, m)
                    if exists(lt) and layer_of(lt) == 1:
                        graph = group_count(lt, m, PER, li)
                        if m is not None:
                            graph = sp.snap(graph)
                        sp.wait_ge(out_added, unit_count(lt, m, PER, li + 1))
                        sp.dma_start(out[bass.ds(graph, 1), :, :].rearrange("b n d -> n (b d)"),
                                     x2[:, li, :]).then_inc(stored[li], 16)
                    if i == 1 and exists(t + 3) and layer_of(t + 3) == 0:
                        load_x(t + 3, m)

            load_x(0, None)
            load_weights(0)
            over_slots(sp, slot)
            for i in range(PER):
                sp.wait_ge(stored[i], 16 * GROUPS)

        @block.gpsimd
        def _(pool):
            count = pool.alloc_register("count")

            def setup(l):
                pool.wait_ge(largest_found, l + 1)
                nc.gpsimd.partition_all_reduce(largest_all[:, :], largest[:, :], P,
                                               bass.bass_isa.ReduceOp.max).then_inc(largest_shared, 1)

            def norm(t, i, m):
                done = unit_count(t, m, PER, i + 1)
                wait_apart(pool, count, mean_found, done)
                nc.gpsimd.tensor_scalar(var_eps[:, :], mean_var[:, 1:2], EPS, HS ** -2, ALU.add,
                                        ALU.mult).then_inc(var_ready, 1)
                pool.wait_ge(var_ready, done)
                nc.gpsimd.tensor_tensor(rstd[:, :], var_eps[:, :], minus_half[:, :], ALU.pow).then_inc(rstd_ready, 1)
                wait_apart(pool, count, rstd_ready, done)
                nc.gpsimd.tensor_scalar(shift[:, :], mean_var[:, 0:1], rstd[:, :], -1.0, ALU.mult,
                                        ALU.mult).then_inc(norm_ready, 1)

            def residual(t, i, m):
                l = layer_of(t)
                xs = (x1 if l else x0)[group_of(t) % 2][:, i, :]
                pool.wait_ge(h_ready, unit_count(t, m, PER, i + 1))
                if unit_no(t) <= 3 and i == 0:
                    pool.wait_ge(out_bias_set, l + 1)
                nc.gpsimd.tensor_tensor(xs, xs, out_bias[l][:, :], ALU.add).then_inc(res_ready, 1)

            def slot(t, m):
                if t == 0:
                    setup(1)
                for i in range(PER):
                    if exists(t + 2):
                        norm(t + 2, i, m)
                        residual(t + 2, i, m)

            nc.gpsimd.memset(minus_half[:, :], -0.5).then_inc(consts_set, 1)
            nc.gpsimd.memset(ones[:, :], 1.0).then_inc(consts_set, 1)
            nc.gpsimd.memset(ident[:, :], 0.0).then_inc(consts_set, 1)
            for b in range(2):
                for vs, one in ((v_hi, 1.0), (v_lo, 0.0)):
                    nc.gpsimd.memset(vs[b][:, :, :, DH:DH + 1], one).then_inc(consts_set, 1)
                    nc.gpsimd.memset(vs[b][:, :, :, DH + 1:VW], 0.0).then_inc(consts_set, 1)
            pool.wait_ge(consts_set, CONSTS)
            nc.gpsimd.affine_select(out=ident[:, :], in_=ident[:, :], compare_op=ALU.not_equal, fill=1.0,
                                    base=0, pattern=[[-1, P]], channel_multiplier=1).then_inc(ident_set, 1)
            setup(0)
            over_slots(pool, slot)

        @block.tensor
        def _(pe):
            def setup(l):
                pe.wait_ge(v_bias_spread, l + 1)
                pe.wait_ge(w_loaded[3], 16 * (l + 1))
                pe.wait_ge(b_loaded, 64 * (l + 1))
                acc = ps_turn[:, 0:H]
                if l:
                    pe.wait_ge(ht_set, unit_count(2, None, PER, 0))
                for c in range(KT):
                    pe.matmul(acc, v_bias_wide[:, c, :], w_raw[3][:, c, :], start=(c == 0), stop=False)
                pe.matmul(acc, ones[0:1, :], f_bias_raw[0:1, :], start=False, stop=True).then_inc(out_bias_summed, 1)

            def three(acc, a_hi, a_lo, b_hi, b_lo, first=True, last=True):
                pe.matmul(acc, a_hi, b_hi, start=first, stop=False)
                pe.matmul(acc, a_hi, b_lo, start=False, stop=False)
                return pe.matmul(acc, a_lo, b_hi, start=False, stop=last)

            def turn_probs(t, i, m):
                pe.wait_ge(exp_done, unit_count(t, m, PER, i + 1))
                for s in range(HEADS):
                    mm = pe.transpose(ps_pt[s // PAIRS][:, (s % PAIRS) * P:(s % PAIRS + 1) * P],
                                      probs[:, s, :], ident[:, :])
                    if s % PAIRS == PAIRS - 1:
                        mm.then_inc(pt_turned, 1)

            def free_bank(t, job, m):
                wait(pe, proj_set, unit_count(t, m, JOBS, job - 1))
                return ps_proj[job % 2]

            def project_v(t, i, m):
                b, l = unit_no(t) % 2, layer_of(t)
                pe.wait_ge(ht_set, unit_count(t, m, PER, i + 1))
                if unit_no(t) <= 3 and i == 0:
                    pe.wait_ge(weights_set, 4 * (l + 1))
                acc = free_bank(t, job_of_v(i), m)[:, 0:H]
                rows = slice(i * NODES, (i + 1) * NODES)
                for c in range(KT):
                    mm = three(acc, ht_hi[b][:, c, rows], ht_lo[b][:, c, rows], w_hi[l][2][:, c, :],
                               w_lo[l][2][:, c, :], c == 0, c == KT - 1)
                mm.then_inc(projected, 1)

            def project_qk(t, chunk, m):
                b, l = unit_no(t) % 2, layer_of(t)
                if chunk == 0:
                    pe.wait_ge(ht_set, unit_count(t, m, PER, PER))
                acc = free_bank(t, job_of_chunk(chunk), m)[:, :]
                which, cols = chunk // KT, slice((chunk % KT) * P, (chunk % KT + 1) * P)
                for c in range(KT):
                    mm = three(acc, w_hi[l][which][:, c, cols], w_lo[l][which][:, c, cols],
                               ht_hi[b][:, c, :], ht_lo[b][:, c, :], c == 0, c == KT - 1)
                mm.then_inc(projected, 1)

            def apply_probs(t, i, m):
                b = unit_no(t) % 2
                wait(pe, out_added, unit_count(t, m, PER, i))
                for s in range(HEADS):
                    if s % PAIRS == 0:
                        pe.wait_ge(pt_set, unit_count(t, m, 2 * PER, 2 * i + 1 + s // PAIRS))
                    hd = head_of(s)
                    mm = three(ps_out[:, hd * VW:(hd + 1) * VW], pt_hi[:, s, :], pt_lo[:, s, :],
                               v_hi[b][:, i, hd, :], v_lo[b][:, i, hd, :])
                mm.then_inc(ctx_summed, 1)

            def score(t, i, m):
                b = unit_no(t) % 2
                if i == 0:
                    pe.wait_ge(proj_set, unit_count(t, m, JOBS, JOBS))
                    pe.wait_ge(mask_set, unit_count(t, m, 1, 1))
                cols = slice(i * NODES, (i + 1) * NODES)
                for c in range(PAIRS):
                    for q, k, first, last in ((qk_hi, qk_hi, True, False), (qk_hi, qk_lo, False, False),
                                              (qk_lo, qk_hi, False, True)):
                        for odd in range(2):
                            rows = slice(odd * DH, (odd + 1) * DH)
                            mm = pe.matmul(ps_scores[odd][:, c * P:(c + 1) * P], q[b][rows, c, cols],
                                           k[b][rows, KT + c, cols], start=first, stop=last)
                mm.then_inc(scored, 1)

            def turn_ctx(t, i, m, preps):
                pe.wait_ge(ctx_ready, unit_count(t, m, PER, i + 1))
                pe.wait_ge(ht_set, preps)
                for c in range(KT):
                    mm = pe.transpose(ps_turn[:, c * P:(c + 1) * P],
                                      ctx_n[:, 2 * c:2 * c + 2, :].rearrange("p a d -> p (a d)"), ident[:, :])
                mm.then_inc(ct_turned, 1)

            def output(t, i, m):
                l = layer_of(t)
                pe.wait_ge(ct_set, unit_count(t, m, PER, i + 1))
                for c in range(KT):
                    mm = three(ps_out[:, 0:H], ct_hi[:, c, :], ct_lo[:, c, :], w_hi[l][3][:, c, :],
                               w_lo[l][3][:, c, :], c == 0, c == KT - 1)
                mm.then_inc(out_summed, 1)

            def turn_h(t, i, m):
                pe.wait_ge(h_ready, unit_count(t, m, PER, i + 1))
                wait(pe, ht_set, unit_count(t, m, PER, i))
                for c in range(KT):
                    mm = pe.transpose(ps_turn[:, c * P:(c + 1) * P], h[:, c * P:(c + 1) * P], ident[:, :])
                mm.then_inc(ht_turned, 1)

            def slot(t, m):
                if t == 0:
                    setup(1)
                for i in range(PER):
                    lt, li = lag_of(t, i)
                    if exists(lt):
                        turn_probs(lt, li, m)
                    if exists(t + 1):
                        project_v(t + 1, i, m)
                    if exists(lt):
                        apply_probs(lt, li, m)
                    if exists(t):
                        score(t, i, m)
                    if exists(lt):
                        turn_ctx(lt, li, m, unit_count(t + 2, m, PER, i if exists(t + 2) else 0))
                    chunks = CHUNKS_OF_STEP[i] if exists(t + 1) else ()
                    for chunk in chunks[:1]:
                        project_qk(t + 1, chunk, m)
                    if exists(lt):
                        output(lt, li, m)
                    for chunk in chunks[1:]:
                        project_qk(t + 1, chunk, m)
                    if exists(t + 2):
                        turn_h(t + 2, i, m)

            pe.wait_ge(ident_set, 1)
            setup(0)
            pe.wait_ge(out_bias_set, 1)
            over_slots(pe, slot)

        @block.scalar
        def _(act):
            def setup(l):
                act.wait_ge(scales_set, l + 1)
                for j in range(4):
                    nc.scalar.activation(w_hi[l][j][:, :, :], w_raw[j][:, :, :], ACT.Copy,
                                         scale=w_scale[:, j:j + 1]).then_inc(w_hi_set, 1)

            def probs_hi(t, i, m):
                for s in range(2):
                    act.wait_ge(pt_turned, unit_count(t, m, 2 * PER, 2 * i + 1 + s))
                    nc.scalar.activation(pt_hi[:, s * PAIRS:(s + 1) * PAIRS, :],
                                         ps_pt[s][:, 0:PAIRS * P].rearrange("p (a k) -> p a k", a=PAIRS),
                                         ACT.Copy).then_inc(pt_hi_set, 1)

            def relu(t, i, m):
                act.wait_ge(norm_ready, unit_count(t, m, PER, i + 1))
                xs = (x1 if layer_of(t) else x0)[group_of(t) % 2][:, i, :]
                nc.scalar.activation(h[:, :], xs, ACT.Relu, bias=shift[:, :], scale=rstd[:, :]).then_inc(h_ready, 1)

            def v_hi_out(t, i, m):
                b, job = unit_no(t) % 2, job_of_v(i)
                act.wait_ge(projected, unit_count(t, m, JOBS, job + 1))
                nc.scalar.activation(v_hi[b][:, i, :, 0:DH],
                                     ps_proj[job % 2][:, 0:H].rearrange("p (a d) -> p a d", a=HEADS),
                                     ACT.Copy).then_inc(proj_hi_set, 1)

            def qk_hi_out(t, chunk, m):
                b, job = unit_no(t) % 2, job_of_chunk(chunk)
                act.wait_ge(projected, unit_count(t, m, JOBS, job + 1))
                nc.scalar.activation(qk_hi[b][:, chunk, :], ps_proj[job % 2][:, :], ACT.Identity,
                                     bias=qk_bias[layer_of(t)][:, chunk // KT, chunk % KT:chunk % KT + 1]
                                     ).then_inc(proj_hi_set, 1)

            def ctx_hi(t, i, m):
                act.wait_ge(ct_turned, unit_count(t, m, PER, i + 1))
                nc.scalar.activation(ct_hi[:, :, :], ps_turn[:, 0:H].rearrange("p (c k) -> p c k", c=KT),
                                     ACT.Copy).then_inc(ct_hi_set, 1)

            def exp(t, i, m):
                act.wait_ge(shifted, unit_count(t, m, PER, i + 1))
                nc.scalar.activation(probs[:, :, :], probs[:, :, :], ACT.Exp,
                                     scale=exp_scale[layer_of(t)][:, :]).then_inc(exp_done, 1)

            def h_hi(t, i, m):
                b = unit_no(t) % 2
                act.wait_ge(ht_turned, unit_count(t, m, PER, i + 1))
                nc.scalar.activation(ht_hi[b][:, :, i * NODES:(i + 1) * NODES],
                                     ps_turn[:, 0:H].rearrange("p (c k) -> p c k", c=KT),
                                     ACT.Copy).then_inc(ht_hi_set, 1)

            def make_mask(t, m):
                b, l = unit_no(t) % 2, layer_of(t)
                act.wait_ge(adj_loaded[b], round_count(t, m, group=False))
                nc.scalar.activation(mask[b][:, :, :], adj_u8[b][:, :, :], ACT.Identity,
                                     bias=mask_shift[l][:, :], scale=mask_scale[l][:, :]).then_inc(mask_set, 1)

            def slot(t, m):
                if t == 0:
                    setup(1)
                for i in range(PER):
                    lt, li = lag_of(t, i)
                    if exists(lt):
                        probs_hi(lt, li, m)
                    if exists(t + 2):
                        relu(t + 2, i, m)
                    if exists(t + 1):
                        v_hi_out(t + 1, i, m)
                    if exists(lt):
                        ctx_hi(lt, li, m)
                    if exists(t):
                        exp(t, i, m)
                    chunks = CHUNKS_OF_STEP[i] if exists(t + 1) else ()
                    if i == 2 and exists(t + 1):
                        make_mask(t + 1, m)
                    for chunk in chunks:
                        qk_hi_out(t + 1, chunk, m)
                    if exists(t + 2):
                        h_hi(t + 2, i, m)

            setup(0)
            over_slots(act, slot)

        @block.vector
        def _(dve):
            count = dve.alloc_register("count")
            chained = [0]

            def then(instruction):
                chained[0] += 1
                instruction.then_inc(setup_chain, 1)
                dve.wait_ge(setup_chain, chained[0])

            def setup(l):
                dve.wait_ge(b_loaded, 64 * (l + 1))
                if l:
                    dve.wait_ge(out_bias_summed, l)
                for c in range(KT):
                    ins = nc.vector.tensor_scalar(v_bias_wide[:, c, :], ones[:, :], v_bias_raw[:, c:c + 1], None,
                                                  ALU.mult)
                ins.then_inc(v_bias_spread, 1)
                nc.vector.tensor_reduce(largest[:, 4:6], qk_bias_raw[:, :, :], AX_X, ALU.max,
                                        apply_absolute_value=True)
                for j in range(4):
                    dve.wait_ge(w_loaded[j], 16 * (l + 1))
                    ins = nc.vector.tensor_reduce(largest[:, j:j + 1],
                                                  w_raw[j][:, :, :].rearrange("p c n -> p (c n)"), AX_X, ALU.max,
                                                  apply_absolute_value=True)
                ins.then_inc(largest_found, 1)
                dve.wait_ge(largest_shared, l + 1)
                then(nc.vector.tensor_scalar(bound[:, 0:3], largest_all[:, 0:3], float(H), LEAST, ALU.mult, ALU.max))
                then(nc.vector.tensor_tensor(bound[:, 0:2], bound[:, 0:2], largest_all[:, 4:6], ALU.add))
                then(nc.vector.tensor_scalar(bound[:, 3:4], largest_all[:, 3:4], LEAST, None, ALU.max))
                then(nc.vector.tensor_scalar(power[:, :].bitcast(I32), bound[:, :].bitcast(I32), 0x7F800000, None,
                                             ALU.bitwise_and))
                then(nc.vector.reciprocal(inverse[:, :], power[:, :]))
                then(nc.vector.tensor_scalar(w_scale[:, 0:3], inverse[:, 0:3], PROJ_TOP, None, ALU.mult))
                then(nc.vector.tensor_scalar(w_scale[:, 3:4], inverse[:, 3:4], OUT_TOP, None, ALU.mult))
                then(nc.vector.tensor_scalar(b_scale[:, :], inverse[:, 0:2], PROJ_TOP * HS, None, ALU.mult))
                then(nc.vector.tensor_tensor(both[:, :], power[:, 0:4:2], power[:, 1:4:2], ALU.mult))
                then(nc.vector.tensor_scalar(exp_scale[l][:, :], both[:, 0:1],
                                             float(DH) ** -0.5 / (PROJ_TOP * HS) ** 2, None, ALU.mult))
                then(nc.vector.tensor_scalar(out_scale[l][:, :], both[:, 1:2], 1.0 / (PROJ_TOP * HS * OUT_TOP), None,
                                             ALU.mult))
                then(nc.vector.reciprocal(exp_inverse[:, :], exp_scale[l][:, :]))
                then(nc.vector.tensor_scalar(mask_scale[l][:, :], exp_inverse[:, :], NEG, None, ALU.mult))
                then(nc.vector.tensor_scalar(mask_shift[l][:, :], exp_inverse[:, :], -NEG, None, ALU.mult))
                for j in range(2):
                    ins = nc.vector.tensor_scalar(qk_bias[l][:, j, :], qk_bias_raw[:, j, :], b_scale[:, j:j + 1],
                                                  None, ALU.mult)
                ins.then_inc(scales_set, 1)
                for j in range(4):
                    dve.wait_ge(w_hi_set, 4 * l + j + 1)
                    nc.vector.scalar_tensor_tensor(out=w_lo[l][j][:, :, :], in0=w_raw[j][:, :, :],
                                                   scalar=w_scale[:, j:j + 1], in1=w_hi[l][j][:, :, :],
                                                   op0=ALU.mult, op1=ALU.subtract).then_inc(weights_set, 1)
                dve.wait_ge(out_bias_summed, l + 1)
                nc.vector.tensor_copy(out_bias[l][:, :], ps_turn[:, 0:H]).then_inc(out_bias_set, 1)

            def statistics(t, i, m):
                done = unit_count(t, m, PER, i + 1)
                g = group_of(t) % 2
                if layer_of(t) == 0 and i == 0:
                    dve.wait_ge(x_loaded[g], round_count(t, m, group=True))
                if layer_of(t) == 1:
                    dve.wait_ge(out_added, unit_count(t - 3, m, PER, i + 1))
                xs = (x1 if layer_of(t) else x0)[g][:, i, :]
                nc.vector.bn_stats(stats[:, :], xs).then_inc(stats_found, 1)
                wait_apart(dve, count, stats_found, done)
                nc.vector.bn_aggr(mean_var[:, :], stats[:, :]).then_inc(mean_found, 1)

            def probs_lo(t, i, m):
                for s in range(2):
                    dve.wait_ge(pt_hi_set, unit_count(t, m, 2 * PER, 2 * i + 1 + s))
                    nc.vector.tensor_tensor(pt_lo[:, s * PAIRS:(s + 1) * PAIRS, :],
                                            ps_pt[s][:, 0:PAIRS * P].rearrange("p (a k) -> p a k", a=PAIRS),
                                            pt_hi[:, s * PAIRS:(s + 1) * PAIRS, :], ALU.subtract
                                            ).then_inc(pt_set, 1)

            def v_lo_out(t, i, m):
                b, job = unit_no(t) % 2, job_of_v(i)
                dve.wait_ge(proj_hi_set, unit_count(t, m, JOBS, job + 1))
                nc.vector.tensor_tensor(v_lo[b][:, i, :, 0:DH],
                                        ps_proj[job % 2][:, 0:H].rearrange("p (a d) -> p a d", a=HEADS),
                                        v_hi[b][:, i, :, 0:DH], ALU.subtract).then_inc(proj_set, 1)

            def qk_lo_out(t, chunk, m):
                b, job = unit_no(t) % 2, job_of_chunk(chunk)
                dve.wait_ge(proj_hi_set, unit_count(t, m, JOBS, job + 1))
                nc.vector.scalar_tensor_tensor(
                    out=qk_lo[b][:, chunk, :], in0=ps_proj[job % 2][:, :],
                    scalar=qk_bias[layer_of(t)][:, chunk // KT, chunk % KT:chunk % KT + 1],
                    in1=qk_hi[b][:, chunk, :], op0=ALU.add, op1=ALU.subtract).then_inc(proj_set, 1)

            def normalise(t, i, m):
                done = unit_count(t, m, PER, i + 1)
                dve.wait_ge(ctx_summed, done)
                summed = ps_out[:, 0:HEADS * VW].rearrange("p (a d) -> p a d", a=HEADS)
                nc.vector.reciprocal(row_rcp[:, :].rearrange("p (a o) -> p a o", o=1),
                                     summed[:, :, DH:DH + 1]).then_inc(rcp_ready, 1)
                dve.wait_ge(rcp_ready, done)
                nc.vector.tensor_tensor(ctx_n[:, :, :], summed[:, :, 0:DH],
                                        row_rcp[:, :].rearrange("p (a o) -> p a o", o=1)
                                        .to_broadcast([P, HEADS, DH]), ALU.mult).then_inc(ctx_ready, 1)

            def mask_and_max(t, i, m):
                b = unit_no(t) % 2
                wait_apart(dve, count, scored, unit_count(t, m, PER, i + 1))
                for s in range(HEADS):
                    ins = nc.vector.tensor_tensor_reduce(
                        probs[:, s, :], ps_scores[s // PAIRS][:, (s % PAIRS) * P:(s % PAIRS + 1) * P],
                        mask[b][:, i, :], 1.0, -3.0e38, ALU.add, ALU.max, row_max[:, s:s + 1])
                ins.then_inc(masked, 1)

            def subtract_max(t, i, m):
                done = unit_count(t, m, PER, i + 1)
                dve.wait_ge(masked, done)
                nc.vector.tensor_tensor(probs[:, :, :], probs[:, :, :],
                                        row_max[:, :].rearrange("p (a o) -> p a o", o=1)
                                        .to_broadcast([P, HEADS, NODES]), ALU.subtract).then_inc(shifted, 1)

            def ctx_lo(t, i, m):
                dve.wait_ge(ct_hi_set, unit_count(t, m, PER, i + 1))
                nc.vector.tensor_tensor(ct_lo[:, :, :], ps_turn[:, 0:H].rearrange("p (c k) -> p c k", c=KT),
                                        ct_hi[:, :, :], ALU.subtract).then_inc(ct_set, 1)

            def add_residual(t, i, m):
                l, g = layer_of(t), group_of(t) % 2
                dve.wait_ge(out_summed, unit_count(t, m, PER, i + 1))
                dve.wait_ge(res_ready, unit_count(t, m, PER, i + 1))
                if l and group_of(t) >= 1:
                    wait(dve, stored[i], group_count(t, m, 16))
                src, dst = (x1[g], x2) if l else (x0[g], x1[g])
                nc.vector.scalar_tensor_tensor(out=dst[:, i, :], in0=ps_out[:, 0:H], scalar=out_scale[l][:, :],
                                               in1=src[:, i, :], op0=ALU.mult, op1=ALU.add).then_inc(out_added, 1)

            def h_lo(t, i, m):
                b = unit_no(t) % 2
                dve.wait_ge(ht_hi_set, unit_count(t, m, PER, i + 1))
                rows = slice(i * NODES, (i + 1) * NODES)
                nc.vector.tensor_tensor(ht_lo[b][:, :, rows], ps_turn[:, 0:H].rearrange("p (c k) -> p c k", c=KT),
                                        ht_hi[b][:, :, rows], ALU.subtract).then_inc(ht_set, 1)

            def slot(t, m):
                if t == 0:
                    setup(1)
                for i in range(PER):
                    lt, li = lag_of(t, i)
                    if exists(t + 2):
                        statistics(t + 2, i, m)
                    if exists(lt):
                        probs_lo(lt, li, m)
                    if exists(t + 1):
                        v_lo_out(t + 1, i, m)
                    if exists(lt):
                        normalise(lt, li, m)
                    if exists(t):
                        mask_and_max(t, i, m)
                    if exists(lt):
                        ctx_lo(lt, li, m)
                    if exists(t):
                        subtract_max(t, i, m)
                    chunks = CHUNKS_OF_STEP[i] if exists(t + 1) else ()
                    for chunk in chunks[:1]:
                        qk_lo_out(t + 1, chunk, m)
                    if exists(lt):
                        add_residual(lt, li, m)
                    for chunk in chunks[1:]:
                        qk_lo_out(t + 1, chunk, m)
                    if exists(t + 2):
                        h_lo(t + 2, i, m)

            dve.wait_ge(consts_set, CONSTS)
            setup(0)
            over_slots(dve, slot)


_WEIGHTS = ("Wq", "bq", "Wk", "bk", "Wv", "bv", "Wf", "bf")


def kernel(**inputs):
    import concourse.bacc as bacc
    from concourse.bass_utils import run_bass_kernel_spmd

    nc = bacc.Bacc("TRN2", target_bir_lowering=False, num_devices=1)
    arrays, aps = {}, {}
    for name, a in inputs.items():
        a = np.ascontiguousarray(a)
        arrays[f"in_{name}"] = a
        aps[name] = nc.dram_tensor(f"in_{name}", a.shape, mybir.dt.from_np(a.dtype), kind="ExternalInput").ap()
    out = nc.dram_tensor("out_x", inputs["x"].shape, F32, kind="ExternalOutput").ap()
    layers = [{w: aps[f"L{l}_gnn_{w}"] for w in _WEIGHTS} for l in range(LAYERS)]
    build(nc, aps["x"], aps["adj"], layers, out)
    r = run_bass_kernel_spmd(nc, [arrays], core_ids=[0])
    return r.results[0]["out_x"]
```

```python
from contextlib import ExitStack

import numpy as np

import concourse.bass as bass
from concourse import mybir

F32 = mybir.dt.float32
F16 = mybir.dt.float16
U8 = mybir.dt.uint8
I32 = mybir.dt.int32
ALU = mybir.AluOpType
ACT = mybir.ActivationFunctionType
AX_X = mybir.AxisListType.X

P = 128
EPS = 1e-5
NEG = 9000000000000000.0
LAYERS = 2


def build(nc, x, adj, layers, out):
    GRAPHS, NODES, H = x.shape
    HEADS = 6
    DH = H // HEADS
    KT = H // P
    PER = 4
    TOK = PER * NODES
    GROUPS = GRAPHS // PER
    VW = DH + 2
    PAIRS = HEADS // 2
    assert NODES == P and GROUPS % 2 == 0

    HS = 4.0
    PROJ_TOP = 2.0 ** 12
    OUT_TOP = 2.0 ** 8
    LEAST = 2.0 ** -20

    FIRST, LAST = -2, 2 * GROUPS + 2
    HOLES = (1, 2 * GROUPS)
    LOOP_AT = 4
    BODY = 4
    CONSTS = 11
    ROUNDS = (2 * GROUPS - 2 - LOOP_AT) // BODY - 0
    JOBS = PER + 2 * KT
    PIECES = (((0, 1), (2, 3), (4,)), ((5, 6), (7, 8), ()), ((9, 10), (11, 12), (13,)), ((14, 15), (16, 17), ()))
    JOB_LIST = (("v", 0, 0), ("qk", 0, 1), ("v", 1, 1), ("qk", 1, 0), ("qk", 2, 1), ("v", 2, 0), ("qk", 3, 1),
                ("v", 3, 1), ("qk", 4, 0), ("qk", 5, 1))
    HELD_BEFORE = (8 - 10, 9 - 10, 1, 0, 2, 3, 4, 6, 5, 7)

    def exists(t):
        return 0 <= t <= LAST - 1 and t not in HOLES

    def unit_no(t):
        return min(t, LAST) - sum(h < t for h in HOLES)

    def layer_of(t):
        return t % 2

    def group_of(t):
        return t // 2 if t % 2 == 0 else (t - 3) // 2

    def job_of(kind, n):
        return next(j for j, job in enumerate(JOB_LIST) if job[:2] == (kind, n))

    def chunks_done(i, part):
        return [p // KT for p in PIECES[i][part] if p % KT == KT - 1]

    def unit_count(t, m, each=1, plus=0):
        return each * unit_no(t) + plus + (m * (each * BODY) if m is not None else 0)

    def group_count(t, m, each=1, plus=0):
        return each * group_of(t) + plus + (m * (each * BODY // 2) if m is not None else 0)

    def round_count(t, m, group, each=16):
        no = group_of(t) if group else unit_no(t)
        per = BODY // 4 if group else BODY // 2
        return each * (no // 2 + 1) + (m * (each * per) if m is not None else 0)

    def wait(eng, sem, value):
        if isinstance(value, int) and value <= 0:
            return
        eng.wait_ge(sem, value)

    def wait_apart(eng, count, sem, value):
        if isinstance(value, int):
            wait(eng, sem, value)
            return
        eng.reg_mov(count, value)
        eng.wait_ge(consts_set, CONSTS)
        eng.wait_ge(sem, count)

    def lag_of(t, i):
        return (t, i - 1) if i else (t - 1, PER - 1)

    def next_of(t, i):
        return (t, i + 1) if i < PER - 1 else (t + 1, 0)

    def over_slots(eng, slot):
        for t in range(FIRST, LOOP_AT):
            slot(t, None)
        with eng.Fori(0, ROUNDS) as m:
            for t in range(LOOP_AT, LOOP_AT + BODY):
                slot(t, m)
        for t in range(LOOP_AT + BODY * ROUNDS, LAST + 1):
            slot(t, None)

    with ExitStack() as ctx:
        def sb(name, shape, dt):
            return ctx.enter_context(nc.sbuf_tensor(name, shape, dt))

        def bank(name):
            return ctx.enter_context(nc.psum_tensor(name, [P, 512], F32))

        def sem(name):
            return ctx.enter_context(nc.semaphore(name))

        NAMES = ("q", "k", "v", "f")
        w_raw = [[sb(f"w{n}_raw{l}", [P, KT, H], F32) for n in NAMES] for l in range(LAYERS)]
        w_hi = [[sb(f"w{n}_hi{l}", [P, KT, H], F16) for n in NAMES] for l in range(LAYERS)]
        w_lo = [[sb(f"w{n}_lo{l}", [P, KT, H], F16) for n in NAMES] for l in range(LAYERS)]
        qk_bias_raw = [sb(f"qk_bias_raw{l}", [P, 2, KT], F32) for l in range(LAYERS)]
        v_bias_raw = [sb(f"v_bias_raw{l}", [P, KT], F32) for l in range(LAYERS)]
        f_bias_raw = [sb(f"f_bias_raw{l}", [1, H], F32) for l in range(LAYERS)]
        qk_bias = [sb(f"qk_bias{l}", [P, 2, KT], F32) for l in range(LAYERS)]
        out_bias = [sb(f"out_bias{l}", [P, H], F32) for l in range(LAYERS)]
        v_bias_wide = sb("v_bias_wide", [P, KT, P], F32)
        ones = sb("ones", [P, P], F32)
        ident = sb("ident", [P, P], F32)
        minus_half = sb("minus_half", [P, 1], F32)
        largest = sb("largest", [P, 6], F32)
        largest_all = sb("largest_all", [P, 6], F32)
        bound = sb("bound", [P, 4], F32)
        power = sb("power", [P, 4], F32)
        inverse = sb("inverse", [P, 4], F32)
        w_scale = sb("w_scale", [P, 4], F32)
        b_scale = sb("b_scale", [P, 2], F32)
        both = sb("both", [P, 2], F32)
        exp_scale = [sb(f"exp_scale{l}", [P, 1], F32) for l in range(LAYERS)]
        out_scale = [sb(f"out_scale{l}", [P, 1], F32) for l in range(LAYERS)]
        exp_inverse = sb("exp_inverse", [P, 1], F32)
        mask_scale = [sb(f"mask_scale{l}", [P, 1], F32) for l in range(LAYERS)]
        mask_shift = [sb(f"mask_shift{l}", [P, 1], F32) for l in range(LAYERS)]

        x0 = [sb(f"x0_{g}", [P, PER, H], F32) for g in range(2)]
        x1 = [sb(f"x1_{g}", [P, PER, H], F32) for g in range(2)]
        x2 = sb("x2", [P, PER, H], F32)
        adj_u8 = [sb(f"adj_u8_{b}", [P, PER, NODES], U8) for b in range(2)]
        mask = [sb(f"mask{b}", [P, PER, NODES], F32) for b in range(2)]
        stats = [sb(f"stats{k}", [P, 6], F32) for k in range(2)]
        mean_var = [sb(f"mean_var{k}", [P, 2], F32) for k in range(2)]
        var_eps = [sb(f"var_eps{k}", [P, 1], F32) for k in range(2)]
        rstd = [sb(f"rstd{k}", [P, 1], F32) for k in range(2)]
        shift = [sb(f"shift{k}", [P, 1], F32) for k in range(2)]
        h = sb("h", [P, H], F32)
        ht_hi = [sb(f"ht_hi{b}", [P, KT, TOK], F16) for b in range(2)]
        ht_lo = [sb(f"ht_lo{b}", [P, KT, TOK], F16) for b in range(2)]
        qk_hi = [sb(f"qk_hi{b}", [P, 2 * KT, TOK], F16) for b in range(2)]
        qk_lo = [sb(f"qk_lo{b}", [P, 2 * KT, TOK], F16) for b in range(2)]
        v_hi = [sb(f"v_hi{b}", [P, PER, HEADS, VW], F16) for b in range(2)]
        v_lo = [sb(f"v_lo{b}", [P, PER, HEADS, VW], F16) for b in range(2)]
        probs = sb("probs", [P, HEADS, NODES], F32)
        row_max = sb("row_max", [P, HEADS], F32)
        pt_hi = sb("pt_hi", [P, HEADS, NODES], F16)
        pt_lo = sb("pt_lo", [P, HEADS, NODES], F16)
        row_rcp = sb("row_rcp", [P, HEADS], F32)
        ctx_n = sb("ctx_n", [P, HEADS, DH], F32)
        ct_hi = sb("ct_hi", [P, KT, NODES], F16)
        ct_lo = sb("ct_lo", [P, KT, NODES], F16)

        ps_scores = [bank("ps_scores0"), bank("ps_scores1")]
        ps_pt = [bank("ps_pt0"), bank("ps_pt1")]
        ps_turn = bank("ps_turn")
        ps_out = bank("ps_out")
        ps_proj = [bank("ps_proj0"), bank("ps_proj1")]

        x_loaded = [sem("x_loaded0"), sem("x_loaded1")]
        adj_loaded = [sem("adj_loaded0"), sem("adj_loaded1")]
        w_loaded = [[sem(f"w{n}_loaded{l}") for n in NAMES] for l in range(LAYERS)]
        b_loaded = [sem("b_loaded0"), sem("b_loaded1")]
        consts_set = sem("consts_set")
        ident_set = sem("ident_set")
        setup_chain = sem("setup_chain")
        largest_found = sem("largest_found")
        largest_shared = sem("largest_shared")
        scales_set = sem("scales_set")
        w_hi_set = sem("w_hi_set")
        weights_set = sem("weights_set")
        v_bias_spread = sem("v_bias_spread")
        out_bias_summed = sem("out_bias_summed")
        out_bias_set = sem("out_bias_set")
        mask_set = sem("mask_set")
        stats_found = sem("stats_found")
        mean_found = sem("mean_found")
        var_ready = sem("var_ready")
        rstd_ready = sem("rstd_ready")
        norm_ready = sem("norm_ready")
        h_ready = sem("h_ready")
        res_ready = sem("res_ready")
        ht_turned = sem("ht_turned")
        ht_hi_set = sem("ht_hi_set")
        ht_set = sem("ht_set")
        projected = sem("projected")
        proj_hi_set = sem("proj_hi_set")
        proj_set = sem("proj_set")
        scored = sem("scored")
        masked = sem("masked")
        shifted = sem("shifted")
        exp_done = sem("exp_done")
        pt_turned = sem("pt_turned")
        pt_hi_set = sem("pt_hi_set")
        pt_set = sem("pt_set")
        ctx_summed = sem("ctx_summed")
        rcp_ready = sem("rcp_ready")
        ctx_ready = sem("ctx_ready")
        ct_turned = sem("ct_turned")
        ct_hi_set = sem("ct_hi_set")
        ct_set = sem("ct_set")
        out_summed = sem("out_summed")
        out_added = sem("out_added")
        stored = [sem(f"stored{i}") for i in range(PER)]

        def head_of(s):
            return 2 * (s % PAIRS) + s // PAIRS

        block = ctx.enter_context(nc.Block())

        @block.sync
        def _(sp):
            count = sp.alloc_register("count")

            def load_x(t, m):
                first = sp.snap(group_count(t, m, PER)) if m is not None else group_count(t, m, PER)
                if group_of(t) >= 2:
                    wait_apart(sp, count, out_added, unit_count(t - 4, m, PER, PER))
                sp.dma_start(x0[group_of(t) % 2][:, :, :],
                             x[bass.ds(first, PER), :, :].rearrange("b n d -> n b d")
                             ).then_inc(x_loaded[group_of(t) % 2], 16)

            def load_adj(t, m):
                first = sp.snap(group_count(t, m, PER)) if m is not None else group_count(t, m, PER)
                if unit_no(t) >= 2:
                    wait_apart(sp, count, mask_set, unit_count(t, m, 1, -1))
                sp.dma_start(adj_u8[unit_no(t) % 2][:, :, :],
                             adj[bass.ds(first, PER), :, :].rearrange("b q k -> q b k")
                             ).then_inc(adj_loaded[unit_no(t) % 2], 16)

            def load_weights(l):
                wts = layers[l]
                with nc.allow_non_contiguous_dma(reason="3 x 384 bias values, once a layer"):
                    for j, b in enumerate(("bq", "bk")):
                        sp.dma_start(qk_bias_raw[l][:, j, :], wts[b].rearrange("(c p) -> p c", p=P)).then_inc(b_loaded[l], 16)
                    sp.dma_start(v_bias_raw[l][:, :], wts["bv"].rearrange("(c p) -> p c", p=P)).then_inc(b_loaded[l], 16)
                sp.dma_start(f_bias_raw[l][:, :], wts["bf"].rearrange("(a n) -> a n", a=1)).then_inc(b_loaded[l], 16)
                for j, w in enumerate(("Wq", "Wk", "Wv", "Wf")):
                    sp.dma_start(w_raw[l][j][:, :, :], wts[w].rearrange("(c p) n -> p c n", p=P)).then_inc(w_loaded[l][j], 16)

            def slot(t, m):
                for i in range(PER):
                    lt, li = lag_of(t, i)
                    if i == 0 and exists(t + 2):
                        load_adj(t + 2, m)
                    if exists(lt) and layer_of(lt) == 1:
                        graph = group_count(lt, m, PER, li)
                        if m is not None:
                            graph = sp.snap(graph)
                        sp.wait_ge(out_added, unit_count(lt, m, PER, li + 1))
                        sp.dma_start(out[bass.ds(graph, 1), :, :].rearrange("b n d -> n (b d)"),
                                     x2[:, li, :]).then_inc(stored[li], 16)
                    if i == 1 and exists(t + 3) and layer_of(t + 3) == 0:
                        load_x(t + 3, m)

            load_x(0, None)
            load_weights(0)
            load_weights(1)
            over_slots(sp, slot)
            for i in range(PER):
                sp.wait_ge(stored[i], 16 * GROUPS)

        @block.gpsimd
        def _(pool):
            count = pool.alloc_register("count")

            def setup(l):
                pool.wait_ge(largest_found, l + 1)
                nc.gpsimd.partition_all_reduce(largest_all[:, :], largest[:, :], P,
                                               bass.bass_isa.ReduceOp.max).then_inc(largest_shared, 1)

            def norm(t, i, m):
                done = unit_count(t, m, PER, i + 1)
                wait_apart(pool, count, mean_found, done)
                nc.gpsimd.tensor_scalar(var_eps[i % 2][:, :], mean_var[i % 2][:, 1:2], EPS, HS ** -2, ALU.add,
                                        ALU.mult).then_inc(var_ready, 1)
                pool.wait_ge(var_ready, done)
                nc.gpsimd.tensor_tensor(rstd[i % 2][:, :], var_eps[i % 2][:, :], minus_half[:, :], ALU.pow).then_inc(rstd_ready, 1)
                wait_apart(pool, count, rstd_ready, done)
                nc.gpsimd.tensor_scalar(shift[i % 2][:, :], mean_var[i % 2][:, 0:1], rstd[i % 2][:, :], -1.0, ALU.mult,
                                        ALU.mult).then_inc(norm_ready, 1)

            def residual(t, i, m):
                l = layer_of(t)
                xs = (x1 if l else x0)[group_of(t) % 2][:, i, :]
                pool.wait_ge(h_ready, unit_count(t, m, PER, i + 1))
                if unit_no(t) <= 3 and i == 0:
                    pool.wait_ge(out_bias_set, l + 1)
                nc.gpsimd.tensor_tensor(xs, xs, out_bias[l][:, :], ALU.add).then_inc(res_ready, 1)

            def slot(t, m):
                if t == -1:
                    setup(1)
                for i in range(PER):
                    nt, ni = next_of(t + 2, i)
                    if exists(nt):
                        norm(nt, ni, m)
                        residual(nt, ni, m)

            nc.gpsimd.memset(minus_half[:, :], -0.5).then_inc(consts_set, 1)
            nc.gpsimd.memset(ones[:, :], 1.0).then_inc(consts_set, 1)
            nc.gpsimd.memset(ident[:, :], 0.0).then_inc(consts_set, 1)
            for b in range(2):
                for vs, one in ((v_hi, 1.0), (v_lo, 0.0)):
                    nc.gpsimd.memset(vs[b][:, :, :, DH:DH + 1], one).then_inc(consts_set, 1)
                    nc.gpsimd.memset(vs[b][:, :, :, DH + 1:VW], 0.0).then_inc(consts_set, 1)
            pool.wait_ge(consts_set, CONSTS)
            nc.gpsimd.affine_select(out=ident[:, :], in_=ident[:, :], compare_op=ALU.not_equal, fill=1.0,
                                    base=0, pattern=[[-1, P]], channel_multiplier=1).then_inc(ident_set, 1)
            setup(0)
            norm(0, 0, None)
            residual(0, 0, None)
            over_slots(pool, slot)

        @block.tensor
        def _(pe):
            def setup(l):
                pe.wait_ge(v_bias_spread, l + 1)
                pe.wait_ge(w_loaded[l][3], 16)
                pe.wait_ge(b_loaded[l], 64)
                acc = ps_pt[l][:, 0:H]
                for c in range(KT):
                    pe.matmul(acc, v_bias_wide[:, c, :], w_raw[l][3][:, c, :], start=(c == 0), stop=False)
                pe.matmul(acc, ones[0:1, :], f_bias_raw[l][0:1, :], start=False, stop=True).then_inc(out_bias_summed, 1)

            def three(acc, a_hi, a_lo, b_hi, b_lo, first=True, last=True):
                pe.matmul(acc, a_hi, b_hi, start=first, stop=False)
                pe.matmul(acc, a_hi, b_lo, start=False, stop=False)
                return pe.matmul(acc, a_lo, b_hi, start=False, stop=last)

            def turn_probs(t, i, m):
                if (t, i) == (0, 0):
                    pe.wait_ge(out_bias_set, LAYERS)
                pe.wait_ge(exp_done, unit_count(t, m, PER, i + 1))
                for s in range(HEADS):
                    mm = pe.transpose(ps_pt[s // PAIRS][:, (s % PAIRS) * P:(s % PAIRS + 1) * P],
                                      probs[:, s, :], ident[:, :])
                    if s % PAIRS == PAIRS - 1:
                        mm.then_inc(pt_turned, 1)

            def free_bank(t, job, m):
                wait(pe, proj_set, unit_count(t, m, JOBS, HELD_BEFORE[job] + 1))

            def project_v(t, i, m):
                b, l = unit_no(t) % 2, layer_of(t)
                pe.wait_ge(ht_set, unit_count(t, m, PER, i + 1))
                if unit_no(t) <= 3 and i == 0:
                    pe.wait_ge(weights_set, 4 * (l + 1))
                job = job_of("v", i)
                free_bank(t, job, m)
                acc = ps_proj[JOB_LIST[job][2]][:, 0:H]
                rows = slice(i * NODES, (i + 1) * NODES)
                for c in range(KT):
                    mm = three(acc, ht_hi[b][:, c, rows], ht_lo[b][:, c, rows], w_hi[l][2][:, c, :],
                               w_lo[l][2][:, c, :], c == 0, c == KT - 1)
                mm.then_inc(projected, 1)

            def project_qk(t, piece, m):
                b, l = unit_no(t) % 2, layer_of(t)
                chunk, c = piece // KT, piece % KT
                job = job_of("qk", chunk)
                if piece == 0:
                    pe.wait_ge(ht_set, unit_count(t, m, PER, PER))
                if c == 0:
                    free_bank(t, job, m)
                which, cols = chunk // KT, slice((chunk % KT) * P, (chunk % KT + 1) * P)
                mm = three(ps_proj[JOB_LIST[job][2]][:, :], w_hi[l][which][:, c, cols], w_lo[l][which][:, c, cols],
                           ht_hi[b][:, c, :], ht_lo[b][:, c, :], c == 0, c == KT - 1)
                if c == KT - 1:
                    mm.then_inc(projected, 1)

            def apply_probs(t, i, m):
                b = unit_no(t) % 2
                wait(pe, out_added, unit_count(t, m, PER, i))
                for s in range(HEADS):
                    if s % PAIRS == 0:
                        pe.wait_ge(pt_set, unit_count(t, m, 2 * PER, 2 * i + 1 + s // PAIRS))
                    hd = head_of(s)
                    mm = three(ps_out[:, hd * VW:(hd + 1) * VW], pt_hi[:, s, :], pt_lo[:, s, :],
                               v_hi[b][:, i, hd, :], v_lo[b][:, i, hd, :])
                mm.then_inc(ctx_summed, 1)

            def score(t, i, m):
                b = unit_no(t) % 2
                if i == 0:
                    pe.wait_ge(proj_set, unit_count(t, m, JOBS, JOBS))
                    pe.wait_ge(mask_set, unit_count(t, m, 1, 1))
                cols = slice(i * NODES, (i + 1) * NODES)
                for c in range(PAIRS):
                    for q, k, first, last in ((qk_hi, qk_hi, True, False), (qk_hi, qk_lo, False, False),
                                              (qk_lo, qk_hi, False, True)):
                        for odd in range(2):
                            rows = slice(odd * DH, (odd + 1) * DH)
                            mm = pe.matmul(ps_scores[odd][:, c * P:(c + 1) * P], q[b][rows, c, cols],
                                           k[b][rows, KT + c, cols], start=first, stop=last)
                mm.then_inc(scored, 1)

            def turn_ctx(t, i, m, preps):
                pe.wait_ge(ctx_ready, unit_count(t, m, PER, i + 1))
                pe.wait_ge(ht_set, preps)
                for c in range(KT):
                    mm = pe.transpose(ps_turn[:, c * P:(c + 1) * P],
                                      ctx_n[:, 2 * c:2 * c + 2, :].rearrange("p a d -> p (a d)"), ident[:, :])
                mm.then_inc(ct_turned, 1)

            def output(t, i, m):
                l = layer_of(t)
                pe.wait_ge(ct_set, unit_count(t, m, PER, i + 1))
                for c in range(KT):
                    mm = three(ps_out[:, 0:H], ct_hi[:, c, :], ct_lo[:, c, :], w_hi[l][3][:, c, :],
                               w_lo[l][3][:, c, :], c == 0, c == KT - 1)
                mm.then_inc(out_summed, 1)

            def turn_h(t, i, m):
                pe.wait_ge(h_ready, unit_count(t, m, PER, i + 1))
                wait(pe, ht_set, unit_count(t, m, PER, i))
                for c in range(KT):
                    mm = pe.transpose(ps_turn[:, c * P:(c + 1) * P], h[:, c * P:(c + 1) * P], ident[:, :])
                mm.then_inc(ht_turned, 1)

            def slot(t, m):
                if t == -1:
                    setup(1)
                for i in range(PER):
                    lt, li = lag_of(t, i)
                    pieces = PIECES[i] if exists(t + 1) else ((), (), ())
                    if exists(lt):
                        turn_probs(lt, li, m)
                    if exists(t):
                        score(t, i, m)
                    if exists(t + 2):
                        turn_h(t + 2, i, m)
                    if exists(t + 1):
                        project_v(t + 1, i, m)
                    if exists(lt):
                        apply_probs(lt, li, m)
                    for piece in pieces[0]:
                        project_qk(t + 1, piece, m)
                    if exists(lt):
                        turn_ctx(lt, li, m, unit_count(t + 2, m, PER, i + 1 if exists(t + 2) else 0))
                    for piece in pieces[1]:
                        project_qk(t + 1, piece, m)
                    if exists(lt):
                        output(lt, li, m)
                    for piece in pieces[2]:
                        project_qk(t + 1, piece, m)

            pe.wait_ge(ident_set, 1)
            setup(0)
            over_slots(pe, slot)

        @block.scalar
        def _(act):
            def setup(l):
                act.wait_ge(scales_set, l + 1)
                for j in range(4):
                    nc.scalar.activation(w_hi[l][j][:, :, :], w_raw[l][j][:, :, :], ACT.Copy,
                                         scale=w_scale[:, j:j + 1]).then_inc(w_hi_set, 1)

            def probs_hi(t, i, m):
                for s in range(2):
                    act.wait_ge(pt_turned, unit_count(t, m, 2 * PER, 2 * i + 1 + s))
                    nc.scalar.activation(pt_hi[:, s * PAIRS:(s + 1) * PAIRS, :],
                                         ps_pt[s][:, 0:PAIRS * P].rearrange("p (a k) -> p a k", a=PAIRS),
                                         ACT.Copy).then_inc(pt_hi_set, 1)

            def relu(t, i, m):
                act.wait_ge(norm_ready, unit_count(t, m, PER, i + 1))
                xs = (x1 if layer_of(t) else x0)[group_of(t) % 2][:, i, :]
                nc.scalar.activation(h[:, :], xs, ACT.Relu, bias=shift[i % 2][:, :], scale=rstd[i % 2][:, :]).then_inc(h_ready, 1)

            def v_hi_out(t, i, m):
                b, job = unit_no(t) % 2, job_of("v", i)
                act.wait_ge(projected, unit_count(t, m, JOBS, job + 1))
                nc.scalar.activation(v_hi[b][:, i, :, 0:DH],
                                     ps_proj[JOB_LIST[job][2]][:, 0:H].rearrange("p (a d) -> p a d", a=HEADS),
                                     ACT.Copy).then_inc(proj_hi_set, 1)

            def qk_hi_out(t, chunk, m):
                b, job = unit_no(t) % 2, job_of("qk", chunk)
                act.wait_ge(projected, unit_count(t, m, JOBS, job + 1))
                nc.scalar.activation(qk_hi[b][:, chunk, :], ps_proj[JOB_LIST[job][2]][:, :], ACT.Identity,
                                     bias=qk_bias[layer_of(t)][:, chunk // KT, chunk % KT:chunk % KT + 1]
                                     ).then_inc(proj_hi_set, 1)

            def ctx_hi(t, i, m):
                act.wait_ge(ct_turned, unit_count(t, m, PER, i + 1))
                nc.scalar.activation(ct_hi[:, :, :], ps_turn[:, 0:H].rearrange("p (c k) -> p c k", c=KT),
                                     ACT.Copy).then_inc(ct_hi_set, 1)

            def exp(t, i, m):
                act.wait_ge(shifted, unit_count(t, m, PER, i + 1))
                nc.scalar.activation(probs[:, :, :], probs[:, :, :], ACT.Exp,
                                     scale=exp_scale[layer_of(t)][:, :]).then_inc(exp_done, 1)

            def h_hi(t, i, m):
                b = unit_no(t) % 2
                act.wait_ge(ht_turned, unit_count(t, m, PER, i + 1))
                nc.scalar.activation(ht_hi[b][:, :, i * NODES:(i + 1) * NODES],
                                     ps_turn[:, 0:H].rearrange("p (c k) -> p c k", c=KT),
                                     ACT.Copy).then_inc(ht_hi_set, 1)

            def make_mask(t, m):
                b, l = unit_no(t) % 2, layer_of(t)
                act.wait_ge(adj_loaded[b], round_count(t, m, group=False))
                nc.scalar.activation(mask[b][:, :, :], adj_u8[b][:, :, :], ACT.Identity,
                                     bias=mask_shift[l][:, :], scale=mask_scale[l][:, :]).then_inc(mask_set, 1)

            def slot(t, m):
                if t == -1:
                    setup(1)
                for i in range(PER):
                    lt, li = lag_of(t, i)
                    nt, ni = next_of(t + 2, i)
                    if exists(lt):
                        probs_hi(lt, li, m)
                    if exists(t + 2):
                        h_hi(t + 2, i, m)
                    if exists(nt):
                        relu(nt, ni, m)
                    if exists(t + 1):
                        v_hi_out(t + 1, i, m)
                        for chunk in chunks_done(i, 0):
                            qk_hi_out(t + 1, chunk, m)
                    if exists(lt):
                        ctx_hi(lt, li, m)
                    if exists(t):
                        exp(t, i, m)
                    if exists(t + 1):
                        for chunk in chunks_done(i, 1) + chunks_done(i, 2):
                            qk_hi_out(t + 1, chunk, m)
                        if i == 2:
                            make_mask(t + 1, m)

            setup(0)
            relu(0, 0, None)
            over_slots(act, slot)

        @block.vector
        def _(dve):
            count = dve.alloc_register("count")
            chained = [0]

            def then(instruction):
                chained[0] += 1
                instruction.then_inc(setup_chain, 1)
                dve.wait_ge(setup_chain, chained[0])

            def setup(l):
                dve.wait_ge(b_loaded[l], 64)
                if l:
                    dve.wait_ge(out_bias_summed, l)
                for c in range(KT):
                    ins = nc.vector.tensor_scalar(v_bias_wide[:, c, :], ones[:, :], v_bias_raw[l][:, c:c + 1], None,
                                                  ALU.mult)
                ins.then_inc(v_bias_spread, 1)
                nc.vector.tensor_reduce(largest[:, 4:6], qk_bias_raw[l][:, :, :], AX_X, ALU.max,
                                        apply_absolute_value=True)
                for j in range(4):
                    dve.wait_ge(w_loaded[l][j], 16)
                    ins = nc.vector.tensor_reduce(largest[:, j:j + 1],
                                                  w_raw[l][j][:, :, :].rearrange("p c n -> p (c n)"), AX_X, ALU.max,
                                                  apply_absolute_value=True)
                ins.then_inc(largest_found, 1)
                dve.wait_ge(largest_shared, l + 1)
                then(nc.vector.tensor_scalar(bound[:, 0:3], largest_all[:, 0:3], float(H), LEAST, ALU.mult, ALU.max))
                then(nc.vector.tensor_tensor(bound[:, 0:2], bound[:, 0:2], largest_all[:, 4:6], ALU.add))
                then(nc.vector.tensor_scalar(bound[:, 3:4], largest_all[:, 3:4], LEAST, None, ALU.max))
                then(nc.vector.tensor_scalar(power[:, :].bitcast(I32), bound[:, :].bitcast(I32), 0x7F800000, None,
                                             ALU.bitwise_and))
                then(nc.vector.reciprocal(inverse[:, :], power[:, :]))
                then(nc.vector.tensor_scalar(w_scale[:, 0:3], inverse[:, 0:3], PROJ_TOP, None, ALU.mult))
                then(nc.vector.tensor_scalar(w_scale[:, 3:4], inverse[:, 3:4], OUT_TOP, None, ALU.mult))
                then(nc.vector.tensor_scalar(b_scale[:, :], inverse[:, 0:2], PROJ_TOP * HS, None, ALU.mult))
                then(nc.vector.tensor_tensor(both[:, :], power[:, 0:4:2], power[:, 1:4:2], ALU.mult))
                then(nc.vector.tensor_scalar(exp_scale[l][:, :], both[:, 0:1],
                                             float(DH) ** -0.5 / (PROJ_TOP * HS) ** 2, None, ALU.mult))
                then(nc.vector.tensor_scalar(out_scale[l][:, :], both[:, 1:2], 1.0 / (PROJ_TOP * HS * OUT_TOP), None,
                                             ALU.mult))
                then(nc.vector.reciprocal(exp_inverse[:, :], exp_scale[l][:, :]))
                then(nc.vector.tensor_scalar(mask_scale[l][:, :], exp_inverse[:, :], NEG, None, ALU.mult))
                then(nc.vector.tensor_scalar(mask_shift[l][:, :], exp_inverse[:, :], -NEG, None, ALU.mult))
                for j in range(2):
                    ins = nc.vector.tensor_scalar(qk_bias[l][:, j, :], qk_bias_raw[l][:, j, :], b_scale[:, j:j + 1],
                                                  None, ALU.mult)
                ins.then_inc(scales_set, 1)
                for j in range(4):
                    dve.wait_ge(w_hi_set, 4 * l + j + 1)
                    nc.vector.scalar_tensor_tensor(out=w_lo[l][j][:, :, :], in0=w_raw[l][j][:, :, :],
                                                   scalar=w_scale[:, j:j + 1], in1=w_hi[l][j][:, :, :],
                                                   op0=ALU.mult, op1=ALU.subtract).then_inc(weights_set, 1)
                dve.wait_ge(out_bias_summed, l + 1)
                nc.vector.tensor_copy(out_bias[l][:, :], ps_pt[l][:, 0:H]).then_inc(out_bias_set, 1)

            def statistics(t, i, m):
                done = unit_count(t, m, PER, i + 1)
                g = group_of(t) % 2
                if layer_of(t) == 0 and i == 0:
                    dve.wait_ge(x_loaded[g], round_count(t, m, group=True))
                if layer_of(t) == 1:
                    dve.wait_ge(out_added, unit_count(t - 3, m, PER, i + 1))
                xs = (x1 if layer_of(t) else x0)[g][:, i, :]
                nc.vector.bn_stats(stats[i % 2][:, :], xs).then_inc(stats_found, 1)
                wait_apart(dve, count, stats_found, done)
                nc.vector.bn_aggr(mean_var[i % 2][:, :], stats[i % 2][:, :]).then_inc(mean_found, 1)

            def probs_lo(t, i, m):
                for s in range(2):
                    dve.wait_ge(pt_hi_set, unit_count(t, m, 2 * PER, 2 * i + 1 + s))
                    nc.vector.tensor_tensor(pt_lo[:, s * PAIRS:(s + 1) * PAIRS, :],
                                            ps_pt[s][:, 0:PAIRS * P].rearrange("p (a k) -> p a k", a=PAIRS),
                                            pt_hi[:, s * PAIRS:(s + 1) * PAIRS, :], ALU.subtract
                                            ).then_inc(pt_set, 1)

            def v_lo_out(t, i, m):
                b, job = unit_no(t) % 2, job_of("v", i)
                dve.wait_ge(proj_hi_set, unit_count(t, m, JOBS, job + 1))
                nc.vector.tensor_tensor(v_lo[b][:, i, :, 0:DH],
                                        ps_proj[JOB_LIST[job][2]][:, 0:H].rearrange("p (a d) -> p a d", a=HEADS),
                                        v_hi[b][:, i, :, 0:DH], ALU.subtract).then_inc(proj_set, 1)

            def qk_lo_out(t, chunk, m):
                b, job = unit_no(t) % 2, job_of("qk", chunk)
                dve.wait_ge(proj_hi_set, unit_count(t, m, JOBS, job + 1))
                nc.vector.scalar_tensor_tensor(
                    out=qk_lo[b][:, chunk, :], in0=ps_proj[JOB_LIST[job][2]][:, :],
                    scalar=qk_bias[layer_of(t)][:, chunk // KT, chunk % KT:chunk % KT + 1],
                    in1=qk_hi[b][:, chunk, :], op0=ALU.add, op1=ALU.subtract).then_inc(proj_set, 1)

            def normalise(t, i, m):
                done = unit_count(t, m, PER, i + 1)
                dve.wait_ge(ctx_summed, done)
                summed = ps_out[:, 0:HEADS * VW].rearrange("p (a d) -> p a d", a=HEADS)
                nc.vector.reciprocal(row_rcp[:, :].rearrange("p (a o) -> p a o", o=1),
                                     summed[:, :, DH:DH + 1]).then_inc(rcp_ready, 1)
                dve.wait_ge(rcp_ready, done)
                nc.vector.tensor_tensor(ctx_n[:, :, :], summed[:, :, 0:DH],
                                        row_rcp[:, :].rearrange("p (a o) -> p a o", o=1)
                                        .to_broadcast([P, HEADS, DH]), ALU.mult).then_inc(ctx_ready, 1)

            def mask_and_max(t, i, m):
                b = unit_no(t) % 2
                wait_apart(dve, count, scored, unit_count(t, m, PER, i + 1))
                for s in range(HEADS):
                    ins = nc.vector.tensor_tensor_reduce(
                        probs[:, s, :], ps_scores[s // PAIRS][:, (s % PAIRS) * P:(s % PAIRS + 1) * P],
                        mask[b][:, i, :], 1.0, -3.0e38, ALU.add, ALU.max, row_max[:, s:s + 1])
                ins.then_inc(masked, 1)

            def subtract_max(t, i, m):
                done = unit_count(t, m, PER, i + 1)
                dve.wait_ge(masked, done)
                nc.vector.tensor_tensor(probs[:, :, :], probs[:, :, :],
                                        row_max[:, :].rearrange("p (a o) -> p a o", o=1)
                                        .to_broadcast([P, HEADS, NODES]), ALU.subtract).then_inc(shifted, 1)

            def ctx_lo(t, i, m):
                dve.wait_ge(ct_hi_set, unit_count(t, m, PER, i + 1))
                nc.vector.tensor_tensor(ct_lo[:, :, :], ps_turn[:, 0:H].rearrange("p (c k) -> p c k", c=KT),
                                        ct_hi[:, :, :], ALU.subtract).then_inc(ct_set, 1)

            def add_residual(t, i, m):
                l, g = layer_of(t), group_of(t) % 2
                dve.wait_ge(out_summed, unit_count(t, m, PER, i + 1))
                dve.wait_ge(res_ready, unit_count(t, m, PER, i + 1))
                if l and group_of(t) >= 1:
                    wait(dve, stored[i], group_count(t, m, 16))
                src, dst = (x1[g], x2) if l else (x0[g], x1[g])
                nc.vector.scalar_tensor_tensor(out=dst[:, i, :], in0=ps_out[:, 0:H], scalar=out_scale[l][:, :],
                                               in1=src[:, i, :], op0=ALU.mult, op1=ALU.add).then_inc(out_added, 1)

            def h_lo(t, i, m):
                b = unit_no(t) % 2
                dve.wait_ge(ht_hi_set, unit_count(t, m, PER, i + 1))
                rows = slice(i * NODES, (i + 1) * NODES)
                nc.vector.tensor_tensor(ht_lo[b][:, :, rows], ps_turn[:, 0:H].rearrange("p (c k) -> p c k", c=KT),
                                        ht_hi[b][:, :, rows], ALU.subtract).then_inc(ht_set, 1)

            def slot(t, m):
                if t == -1:
                    setup(1)
                for i in range(PER):
                    lt, li = lag_of(t, i)
                    nt, ni = next_of(t + 2, i)
                    if exists(nt):
                        statistics(nt, ni, m)
                    if exists(lt):
                        probs_lo(lt, li, m)
                    if exists(t):
                        mask_and_max(t, i, m)
                    if exists(t + 2):
                        h_lo(t + 2, i, m)
                    if exists(t + 1):
                        v_lo_out(t + 1, i, m)
                    if exists(lt):
                        normalise(lt, li, m)
                    if exists(t):
                        subtract_max(t, i, m)
                    if exists(lt):
                        ctx_lo(lt, li, m)
                    if exists(t + 1):
                        for chunk in chunks_done(i, 0) + chunks_done(i, 1) + chunks_done(i, 2):
                            qk_lo_out(t + 1, chunk, m)
                    if exists(lt):
                        add_residual(lt, li, m)

            dve.wait_ge(consts_set, CONSTS)
            setup(0)
            statistics(0, 0, None)
            over_slots(dve, slot)


_WEIGHTS = ("Wq", "bq", "Wk", "bk", "Wv", "bv", "Wf", "bf")


def kernel(**inputs):
    import concourse.bacc as bacc
    from concourse.bass_utils import run_bass_kernel_spmd

    nc = bacc.Bacc("TRN2", target_bir_lowering=False, num_devices=1)
    arrays, aps = {}, {}
    for name, a in inputs.items():
        a = np.ascontiguousarray(a)
        arrays[f"in_{name}"] = a
        aps[name] = nc.dram_tensor(f"in_{name}", a.shape, mybir.dt.from_np(a.dtype), kind="ExternalInput").ap()
    out = nc.dram_tensor("out_x", inputs["x"].shape, F32, kind="ExternalOutput").ap()
    layers = [{w: aps[f"L{l}_gnn_{w}"] for w in _WEIGHTS} for l in range(LAYERS)]
    build(nc, aps["x"], aps["adj"], layers, out)
    r = run_bass_kernel_spmd(nc, [arrays], core_ids=[0])
    return r.results[0]["out_x"]
```

```python
from contextlib import ExitStack

import numpy as np

import concourse.bass as bass
from concourse import mybir

F32 = mybir.dt.float32
F16 = mybir.dt.float16
U8 = mybir.dt.uint8
I32 = mybir.dt.int32
ALU = mybir.AluOpType
ACT = mybir.ActivationFunctionType
AX_X = mybir.AxisListType.X

P = 128
EPS = 1e-5
NEG = 9000000000000000.0
LAYERS = 2


def build(nc, x, adj, layers, out):
    GRAPHS, NODES, H = x.shape
    HEADS = 6
    DH = H // HEADS
    KT = H // P
    PER = 4
    TOK = PER * NODES
    GROUPS = GRAPHS // PER
    VW = DH + 2
    PAIRS = HEADS // 2
    assert NODES == P and GROUPS % 2 == 0

    HS = 4.0
    PROJ_TOP = 2.0 ** 12
    OUT_TOP = 2.0 ** 8
    LEAST = 2.0 ** -20

    FIRST, LAST = -2, LAYERS * GROUPS
    AHEAD = 3
    LOOP_AT = 5
    BODY = 8
    ROUNDS = (LAST - 5 - LOOP_AT) // BODY
    X1_BUFFERS = BODY // 2
    CONSTS = 11
    JOBS = PER + 2 * KT
    PIECES = (((0, 1), (2, 3), (4,)), ((5, 6), (7, 8), ()), ((9, 10), (11, 12), (13,)), ((14, 15), (16, 17), ()))
    JOB_LIST = (("v", 0, 0), ("qk", 0, 1), ("v", 1, 1), ("qk", 1, 0), ("qk", 2, 1), ("v", 2, 0), ("qk", 3, 1),
                ("v", 3, 1), ("qk", 4, 0), ("qk", 5, 1))
    HELD_BEFORE = (8 - 10, 9 - 10, 1, 0, 2, 3, 4, 6, 5, 7)

    def exists(t):
        return 0 <= t <= LAST - 1

    def unit_no(t):
        return min(t, LAST)

    def layer_of(t):
        return 0 if t < AHEAD else 1 if t >= LAST - 2 else t % 2

    def group_of(t):
        if t < AHEAD:
            return t
        if t >= LAST - 2:
            return t - LAST + GROUPS
        return (t - 3) // 2 if t % 2 else (t + 2) // 2

    def first_layer_slot(group):
        return group if group < AHEAD else 2 * group - 2

    def job_of(kind, n):
        return next(j for j, job in enumerate(JOB_LIST) if job[:2] == (kind, n))

    def chunks_done(i, part):
        return [p // KT for p in PIECES[i][part] if p % KT == KT - 1]

    def unit_count(t, m, each=1, plus=0):
        return each * unit_no(t) + plus + (m * (each * BODY) if m is not None else 0)

    def group_count(t, m, each=1, plus=0):
        return each * group_of(t) + plus + (m * (each * BODY // 2) if m is not None else 0)

    def adj_count(t, m):
        return 16 * (unit_no(t) // 2 + 1) + (m * (16 * BODY // 2) if m is not None else 0)

    def x_buffer(group):
        return group if group < AHEAD else (group - AHEAD) % 2

    def x_count(group, m):
        return 16 * (1 if group < AHEAD else (group + 1) // 2) + (m * (16 * BODY // 4) if m is not None else 0)

    def wait(eng, sem, value):
        if isinstance(value, int) and value <= 0:
            return
        eng.wait_ge(sem, value)

    def wait_apart(eng, count, sem, value):
        if isinstance(value, int):
            wait(eng, sem, value)
            return
        eng.reg_mov(count, value)
        eng.wait_ge(consts_set, CONSTS)
        eng.wait_ge(sem, count)

    def lag_of(t, i):
        return (t, i - 1) if i else (t - 1, PER - 1)

    def next_of(t, i):
        return (t, i + 1) if i < PER - 1 else (t + 1, 0)

    def over_slots(eng, slot):
        for t in range(FIRST + 1, LOOP_AT):
            slot(t, None)
        with eng.Fori(0, ROUNDS) as m:
            for t in range(LOOP_AT, LOOP_AT + BODY):
                slot(t, m)
        for t in range(LOOP_AT + BODY * ROUNDS, LAST + 1):
            slot(t, None)

    with ExitStack() as ctx:
        def sb(name, shape, dt):
            return ctx.enter_context(nc.sbuf_tensor(name, shape, dt))

        def bank(name):
            return ctx.enter_context(nc.psum_tensor(name, [P, 512], F32))

        def sem(name):
            return ctx.enter_context(nc.semaphore(name))

        NAMES = ("q", "k", "v", "f")
        w_raw = [[sb(f"w{n}_raw{l}", [P, KT, H], F32) for n in NAMES] for l in range(LAYERS)]
        w_hi = [[sb(f"w{n}_hi{l}", [P, KT, H], F16) for n in NAMES] for l in range(LAYERS)]
        w_lo = [[sb(f"w{n}_lo{l}", [P, KT, H], F16) for n in NAMES] for l in range(LAYERS)]
        qk_bias_raw = [sb(f"qk_bias_raw{l}", [P, 2, KT], F32) for l in range(LAYERS)]
        v_bias_raw = [sb(f"v_bias_raw{l}", [P, KT], F32) for l in range(LAYERS)]
        f_bias_raw = [sb(f"f_bias_raw{l}", [1, H], F32) for l in range(LAYERS)]
        qk_bias = [sb(f"qk_bias{l}", [P, 2, KT], F32) for l in range(LAYERS)]
        out_bias = [sb(f"out_bias{l}", [P, H], F32) for l in range(LAYERS)]
        v_bias_wide = sb("v_bias_wide", [P, KT, P], F32)
        ones = sb("ones", [P, P], F32)
        ident = sb("ident", [P, P], F32)
        minus_half = sb("minus_half", [P, 1], F32)
        largest = sb("largest", [P, 6], F32)
        largest_all = sb("largest_all", [P, 6], F32)
        bound = sb("bound", [P, 4], F32)
        power = sb("power", [P, 4], F32)
        inverse = sb("inverse", [P, 4], F32)
        w_scale = [sb(f"w_scale{l}", [P, 4], F32) for l in range(LAYERS)]
        b_scale = sb("b_scale", [P, 2], F32)
        both = sb("both", [P, 2], F32)
        exp_scale = [sb(f"exp_scale{l}", [P, 1], F32) for l in range(LAYERS)]
        out_scale = [sb(f"out_scale{l}", [P, 1], F32) for l in range(LAYERS)]
        exp_inverse = sb("exp_inverse", [P, 1], F32)
        mask_scale = [sb(f"mask_scale{l}", [P, 1], F32) for l in range(LAYERS)]
        mask_shift = [sb(f"mask_shift{l}", [P, 1], F32) for l in range(LAYERS)]

        x0 = [sb(f"x0_{g}", [P, PER, H], F32) for g in range(2)]
        x1 = [sb(f"x1_{g}", [P, PER, H], F32) for g in range(X1_BUFFERS)]
        x2 = sb("x2", [P, PER, H], F32)
        adj_u8 = [sb(f"adj_u8_{b}", [P, PER, NODES], U8) for b in range(2)]
        mask = [sb(f"mask{b}", [P, PER, NODES], F32) for b in range(2)]
        stats = [sb(f"stats{k}", [P, 6], F32) for k in range(2)]
        mean_var = [sb(f"mean_var{k}", [P, 2], F32) for k in range(2)]
        var_eps = [sb(f"var_eps{k}", [P, 1], F32) for k in range(2)]
        rstd = [sb(f"rstd{k}", [P, 1], F32) for k in range(2)]
        shift = [sb(f"shift{k}", [P, 1], F32) for k in range(2)]
        h = sb("h", [P, H], F32)
        ht_hi = [sb(f"ht_hi{b}", [P, KT, TOK], F16) for b in range(2)]
        ht_lo = [sb(f"ht_lo{b}", [P, KT, TOK], F16) for b in range(2)]
        qk_hi = [sb(f"qk_hi{b}", [P, 2 * KT, TOK], F16) for b in range(2)]
        qk_lo = [sb(f"qk_lo{b}", [P, 2 * KT, TOK], F16) for b in range(2)]
        v_hi = [sb(f"v_hi{b}", [P, PER, HEADS, VW], F16) for b in range(2)]
        v_lo = [sb(f"v_lo{b}", [P, PER, HEADS, VW], F16) for b in range(2)]
        probs = sb("probs", [P, HEADS, NODES], F32)
        row_max = sb("row_max", [P, HEADS], F32)
        pt_hi = sb("pt_hi", [P, HEADS, NODES], F16)
        pt_lo = sb("pt_lo", [P, HEADS, NODES], F16)
        row_rcp = sb("row_rcp", [P, HEADS], F32)
        ctx_n = sb("ctx_n", [P, HEADS, DH], F32)
        ct_hi = sb("ct_hi", [P, KT, NODES], F16)
        ct_lo = sb("ct_lo", [P, KT, NODES], F16)

        ps_scores = [bank("ps_scores0"), bank("ps_scores1")]
        ps_pt = [bank("ps_pt0"), bank("ps_pt1")]
        ps_turn = bank("ps_turn")
        ps_out = bank("ps_out")
        ps_proj = [bank("ps_proj0"), bank("ps_proj1")]
        CAST_ORDER = (2, 0, 1, 3)

        x_loaded = [sem(f"x_loaded{b}") for b in range(3)]
        adj_loaded = [sem("adj_loaded0"), sem("adj_loaded1")]
        w_loaded = [[sem(f"w{n}_loaded{l}") for n in NAMES] for l in range(LAYERS)]
        b_loaded = [sem("b_loaded0"), sem("b_loaded1")]
        consts_set = sem("consts_set")
        ident_set = sem("ident_set")
        setup_chain = sem("setup_chain")
        largest_found = sem("largest_found")
        largest_shared = sem("largest_shared")
        scales_set = sem("scales_set")
        w_hi_set = sem("w_hi_set")
        weights_set = sem("weights_set")
        v_bias_spread = sem("v_bias_spread")
        out_bias_summed = sem("out_bias_summed")
        out_bias_set = sem("out_bias_set")
        mask_set = sem("mask_set")
        stats_found = sem("stats_found")
        mean_found = sem("mean_found")
        var_ready = sem("var_ready")
        rstd_ready = sem("rstd_ready")
        norm_ready = sem("norm_ready")
        h_ready = sem("h_ready")
        res_ready = sem("res_ready")
        ht_turned = sem("ht_turned")
        ht_hi_set = sem("ht_hi_set")
        ht_set = sem("ht_set")
        projected = sem("projected")
        proj_hi_set = sem("proj_hi_set")
        proj_set = sem("proj_set")
        scored = sem("scored")
        masked = sem("masked")
        shifted = sem("shifted")
        exp_done = sem("exp_done")
        pt_turned = sem("pt_turned")
        pt_hi_set = sem("pt_hi_set")
        pt_set = sem("pt_set")
        ctx_summed = sem("ctx_summed")
        rcp_ready = sem("rcp_ready")
        ctx_ready = sem("ctx_ready")
        ct_turned = sem("ct_turned")
        ct_hi_set = sem("ct_hi_set")
        ct_set = sem("ct_set")
        out_summed = sem("out_summed")
        out_added = sem("out_added")
        stored = [sem(f"stored{i}") for i in range(PER)]

        def x_of(t):
            g = group_of(t)
            return x1[g % X1_BUFFERS] if layer_of(t) else (x0 + [x2])[x_buffer(g)]

        def head_of(s):
            return 2 * (s % PAIRS) + s // PAIRS

        block = ctx.enter_context(nc.Block())

        @block.sync
        def _(sp):
            count = sp.alloc_register("count")

            def load_x(t, m):
                first = sp.snap(group_count(t, m, PER)) if m is not None else group_count(t, m, PER)
                g = group_of(t)
                if g >= AHEAD:
                    wait_apart(sp, count, out_added, unit_count(t - 4, m, PER, PER))
                sp.dma_start(x_of(t)[:, :, :], x[bass.ds(first, PER), :, :].rearrange("b n d -> n b d")
                             ).then_inc(x_loaded[x_buffer(g)], 16)

            def load_adj(t, m):
                first = sp.snap(group_count(t, m, PER)) if m is not None else group_count(t, m, PER)
                if unit_no(t) >= 2:
                    wait_apart(sp, count, mask_set, unit_count(t, m, 1, -1))
                sp.dma_start(adj_u8[unit_no(t) % 2][:, :, :],
                             adj[bass.ds(first, PER), :, :].rearrange("b q k -> q b k")
                             ).then_inc(adj_loaded[unit_no(t) % 2], 16)

            def load_weights(l):
                wts = layers[l]
                with nc.allow_non_contiguous_dma(reason="3 x 384 bias values, once a layer"):
                    for j, b in enumerate(("bq", "bk")):
                        sp.dma_start(qk_bias_raw[l][:, j, :], wts[b].rearrange("(c p) -> p c", p=P)).then_inc(b_loaded[l], 16)
                    sp.dma_start(v_bias_raw[l][:, :], wts["bv"].rearrange("(c p) -> p c", p=P)).then_inc(b_loaded[l], 16)
                sp.dma_start(f_bias_raw[l][:, :], wts["bf"].rearrange("(a n) -> a n", a=1)).then_inc(b_loaded[l], 16)
                for j, w in enumerate(("Wq", "Wk", "Wv", "Wf")):
                    sp.dma_start(w_raw[l][j][:, :, :], wts[w].rearrange("(c p) n -> p c n", p=P)).then_inc(w_loaded[l][j], 16)

            def slot(t, m):
                for i in range(PER):
                    lt, li = lag_of(t, i)
                    if i == 0 and exists(t + 2):
                        load_adj(t + 2, m)
                    if exists(lt) and layer_of(lt) == 1:
                        graph = group_count(lt, m, PER, li)
                        if m is not None:
                            graph = sp.snap(graph)
                        sp.wait_ge(out_added, unit_count(lt, m, PER, li + 1))
                        sp.dma_start(out[bass.ds(graph, 1), :, :].rearrange("b n d -> n (b d)"),
                                     x2[:, li, :]).then_inc(stored[li], 16)
                    if i == 1 and exists(t + 3) and layer_of(t + 3) == 0:
                        load_x(t + 3, m)

            load_x(0, None)
            load_weights(0)
            slot(FIRST, None)
            load_weights(1)
            over_slots(sp, slot)
            for i in range(PER):
                sp.wait_ge(stored[i], 16 * GROUPS)

        @block.gpsimd
        def _(pool):
            count = pool.alloc_register("count")

            def setup(l):
                pool.wait_ge(largest_found, 5 * (l + 1))
                nc.gpsimd.partition_all_reduce(largest_all[:, :], largest[:, :], P,
                                               bass.bass_isa.ReduceOp.max).then_inc(largest_shared, 1)

            def norm(t, i, m):
                done = unit_count(t, m, PER, i + 1)
                wait_apart(pool, count, mean_found, done)
                nc.gpsimd.tensor_scalar(var_eps[i % 2][:, :], mean_var[i % 2][:, 1:2], EPS, HS ** -2, ALU.add,
                                        ALU.mult).then_inc(var_ready, 1)
                pool.wait_ge(var_ready, done)
                nc.gpsimd.tensor_tensor(rstd[i % 2][:, :], var_eps[i % 2][:, :], minus_half[:, :], ALU.pow).then_inc(rstd_ready, 1)
                wait_apart(pool, count, rstd_ready, done)
                nc.gpsimd.tensor_scalar(shift[i % 2][:, :], mean_var[i % 2][:, 0:1], rstd[i % 2][:, :], -1.0, ALU.mult,
                                        ALU.mult).then_inc(norm_ready, 1)

            def residual(t, i, m):
                l = layer_of(t)
                xs = x_of(t)[:, i, :]
                pool.wait_ge(h_ready, unit_count(t, m, PER, i + 1))
                if unit_no(t) <= 3 and i == 0:
                    pool.wait_ge(out_bias_set, l + 1)
                nc.gpsimd.tensor_tensor(xs, xs, out_bias[l][:, :], ALU.add).then_inc(res_ready, 1)

            def slot(t, m):
                for i in range(PER):
                    nt, ni = next_of(t + 2, i)
                    if (t, i) == (FIRST, 3):
                        setup(0)
                    if (t, i) == (0, 1):
                        setup(1)
                    if exists(nt):
                        norm(nt, ni, m)
                    if exists(t + 1):
                        residual(t + 1, i, m)

            nc.gpsimd.memset(minus_half[:, :], -0.5).then_inc(consts_set, 1)
            nc.gpsimd.memset(ones[:, :], 1.0).then_inc(consts_set, 1)
            nc.gpsimd.memset(ident[:, :], 0.0).then_inc(consts_set, 1)
            for b in range(2):
                for vs, one in ((v_hi, 1.0), (v_lo, 0.0)):
                    nc.gpsimd.memset(vs[b][:, :, :, DH:DH + 1], one).then_inc(consts_set, 1)
                    nc.gpsimd.memset(vs[b][:, :, :, DH + 1:VW], 0.0).then_inc(consts_set, 1)
            pool.wait_ge(consts_set, CONSTS)
            nc.gpsimd.affine_select(out=ident[:, :], in_=ident[:, :], compare_op=ALU.not_equal, fill=1.0,
                                    base=0, pattern=[[-1, P]], channel_multiplier=1).then_inc(ident_set, 1)
            norm(0, 0, None)
            slot(FIRST, None)
            over_slots(pool, slot)

        @block.tensor
        def _(pe):
            def setup(l):
                pe.wait_ge(v_bias_spread, l + 1)
                pe.wait_ge(w_loaded[l][3], 16)
                pe.wait_ge(b_loaded[l], 64)
                acc = ps_pt[l][:, 0:H]
                for c in range(KT):
                    pe.matmul(acc, v_bias_wide[:, c, :], w_raw[l][3][:, c, :], start=(c == 0), stop=False)
                pe.matmul(acc, ones[0:1, :], f_bias_raw[l][0:1, :], start=False, stop=True).then_inc(out_bias_summed, 1)

            def three(acc, a_hi, a_lo, b_hi, b_lo, first=True, last=True):
                pe.matmul(acc, a_hi, b_hi, start=first, stop=False)
                pe.matmul(acc, a_hi, b_lo, start=False, stop=False)
                return pe.matmul(acc, a_lo, b_hi, start=False, stop=last)

            def turn_probs(t, i, m):
                if (t, i) == (0, 0):
                    pe.wait_ge(out_bias_set, LAYERS)
                pe.wait_ge(exp_done, unit_count(t, m, PER, i + 1))
                for s in range(HEADS):
                    mm = pe.transpose(ps_pt[s // PAIRS][:, (s % PAIRS) * P:(s % PAIRS + 1) * P],
                                      probs[:, s, :], ident[:, :])
                    if s % PAIRS == PAIRS - 1:
                        mm.then_inc(pt_turned, 1)

            def free_bank(t, job, m):
                wait(pe, proj_set, unit_count(t, m, JOBS, HELD_BEFORE[job] + 1))

            def project_v(t, i, m):
                b, l = unit_no(t) % 2, layer_of(t)
                pe.wait_ge(ht_set, unit_count(t, m, PER, i + 1))
                if unit_no(t) <= 3 and i == 0:
                    pe.wait_ge(weights_set, 4 * l + 1)
                job = job_of("v", i)
                free_bank(t, job, m)
                acc = ps_proj[JOB_LIST[job][2]][:, 0:H]
                rows = slice(i * NODES, (i + 1) * NODES)
                for c in range(KT):
                    mm = three(acc, ht_hi[b][:, c, rows], ht_lo[b][:, c, rows], w_hi[l][2][:, c, :],
                               w_lo[l][2][:, c, :], c == 0, c == KT - 1)
                mm.then_inc(projected, 1)

            def project_qk(t, piece, m):
                b, l = unit_no(t) % 2, layer_of(t)
                chunk, c = piece // KT, piece % KT
                job = job_of("qk", chunk)
                if piece == 0:
                    pe.wait_ge(ht_set, unit_count(t, m, PER, PER))
                    if unit_no(t) <= 3:
                        pe.wait_ge(weights_set, 4 * (l + 1))
                if c == 0:
                    free_bank(t, job, m)
                which, cols = chunk // KT, slice((chunk % KT) * P, (chunk % KT + 1) * P)
                mm = three(ps_proj[JOB_LIST[job][2]][:, :], w_hi[l][which][:, c, cols], w_lo[l][which][:, c, cols],
                           ht_hi[b][:, c, :], ht_lo[b][:, c, :], c == 0, c == KT - 1)
                if c == KT - 1:
                    mm.then_inc(projected, 1)

            def apply_probs(t, i, m):
                b = unit_no(t) % 2
                wait(pe, out_added, unit_count(t, m, PER, i))
                for s in range(HEADS):
                    if s % PAIRS == 0:
                        pe.wait_ge(pt_set, unit_count(t, m, 2 * PER, 2 * i + 1 + s // PAIRS))
                    hd = head_of(s)
                    mm = three(ps_out[:, hd * VW:(hd + 1) * VW], pt_hi[:, s, :], pt_lo[:, s, :],
                               v_hi[b][:, i, hd, :], v_lo[b][:, i, hd, :])
                mm.then_inc(ctx_summed, 1)

            def score(t, i, m):
                b = unit_no(t) % 2
                if i == 0:
                    pe.wait_ge(proj_set, unit_count(t, m, JOBS, JOBS))
                    pe.wait_ge(mask_set, unit_count(t, m, 1, 1))
                cols = slice(i * NODES, (i + 1) * NODES)
                for c in range(PAIRS):
                    for q, k, first, last in ((qk_hi, qk_hi, True, False), (qk_hi, qk_lo, False, False),
                                              (qk_lo, qk_hi, False, True)):
                        for odd in range(2):
                            rows = slice(odd * DH, (odd + 1) * DH)
                            mm = pe.matmul(ps_scores[odd][:, c * P:(c + 1) * P], q[b][rows, c, cols],
                                           k[b][rows, KT + c, cols], start=first, stop=last)
                mm.then_inc(scored, 1)

            def turn_ctx(t, i, m, preps):
                pe.wait_ge(ctx_ready, unit_count(t, m, PER, i + 1))
                pe.wait_ge(ht_set, preps)
                for c in range(KT):
                    mm = pe.transpose(ps_turn[:, c * P:(c + 1) * P],
                                      ctx_n[:, 2 * c:2 * c + 2, :].rearrange("p a d -> p (a d)"), ident[:, :])
                mm.then_inc(ct_turned, 1)

            def output(t, i, m):
                l = layer_of(t)
                pe.wait_ge(ct_set, unit_count(t, m, PER, i + 1))
                for c in range(KT):
                    mm = three(ps_out[:, 0:H], ct_hi[:, c, :], ct_lo[:, c, :], w_hi[l][3][:, c, :],
                               w_lo[l][3][:, c, :], c == 0, c == KT - 1)
                mm.then_inc(out_summed, 1)

            def turn_h(t, i, m):
                pe.wait_ge(h_ready, unit_count(t, m, PER, i + 1))
                wait(pe, ht_set, unit_count(t, m, PER, i))
                for c in range(KT):
                    mm = pe.transpose(ps_turn[:, c * P:(c + 1) * P], h[:, c * P:(c + 1) * P], ident[:, :])
                mm.then_inc(ht_turned, 1)

            def slot(t, m):
                for i in range(PER):
                    lt, li = lag_of(t, i)
                    pieces = PIECES[i] if exists(t + 1) else ((), (), ())
                    if exists(lt):
                        turn_probs(lt, li, m)
                    if exists(t):
                        score(t, i, m)
                    if exists(t + 2):
                        turn_h(t + 2, i, m)
                    if exists(t + 1):
                        project_v(t + 1, i, m)
                    if exists(lt):
                        apply_probs(lt, li, m)
                    if (t, i) == (-1, 2):
                        setup(1)
                    for piece in pieces[0]:
                        project_qk(t + 1, piece, m)
                    if exists(lt):
                        turn_ctx(lt, li, m, unit_count(t + 2, m, PER, i + 1 if exists(t + 2) else 0))
                    for piece in pieces[1]:
                        project_qk(t + 1, piece, m)
                    if exists(lt):
                        output(lt, li, m)
                    for piece in pieces[2]:
                        project_qk(t + 1, piece, m)

            pe.wait_ge(ident_set, 1)
            slot(FIRST, None)
            setup(0)
            over_slots(pe, slot)

        @block.scalar
        def _(act):
            def weights_hi(l, j):
                act.wait_ge(scales_set, l + 1)
                nc.scalar.activation(w_hi[l][j][:, :, :], w_raw[l][j][:, :, :], ACT.Copy,
                                     scale=w_scale[l][:, j:j + 1]).then_inc(w_hi_set, 1)

            def probs_hi(t, i, m):
                for s in range(2):
                    act.wait_ge(pt_turned, unit_count(t, m, 2 * PER, 2 * i + 1 + s))
                    nc.scalar.activation(pt_hi[:, s * PAIRS:(s + 1) * PAIRS, :],
                                         ps_pt[s][:, 0:PAIRS * P].rearrange("p (a k) -> p a k", a=PAIRS),
                                         ACT.Copy).then_inc(pt_hi_set, 1)

            def relu(t, i, m):
                act.wait_ge(norm_ready, unit_count(t, m, PER, i + 1))
                xs = x_of(t)[:, i, :]
                nc.scalar.activation(h[:, :], xs, ACT.Relu, bias=shift[i % 2][:, :], scale=rstd[i % 2][:, :]).then_inc(h_ready, 1)

            def v_hi_out(t, i, m):
                b, job = unit_no(t) % 2, job_of("v", i)
                act.wait_ge(projected, unit_count(t, m, JOBS, job + 1))
                nc.scalar.activation(v_hi[b][:, i, :, 0:DH],
                                     ps_proj[JOB_LIST[job][2]][:, 0:H].rearrange("p (a d) -> p a d", a=HEADS),
                                     ACT.Copy).then_inc(proj_hi_set, 1)

            def qk_hi_out(t, chunk, m):
                b, job = unit_no(t) % 2, job_of("qk", chunk)
                act.wait_ge(projected, unit_count(t, m, JOBS, job + 1))
                nc.scalar.activation(qk_hi[b][:, chunk, :], ps_proj[JOB_LIST[job][2]][:, :], ACT.Identity,
                                     bias=qk_bias[layer_of(t)][:, chunk // KT, chunk % KT:chunk % KT + 1]
                                     ).then_inc(proj_hi_set, 1)

            def ctx_hi(t, i, m):
                act.wait_ge(ct_turned, unit_count(t, m, PER, i + 1))
                nc.scalar.activation(ct_hi[:, :, :], ps_turn[:, 0:H].rearrange("p (c k) -> p c k", c=KT),
                                     ACT.Copy).then_inc(ct_hi_set, 1)

            def exp(t, i, m):
                act.wait_ge(shifted, unit_count(t, m, PER, i + 1))
                nc.scalar.activation(probs[:, :, :], probs[:, :, :], ACT.Exp,
                                     scale=exp_scale[layer_of(t)][:, :]).then_inc(exp_done, 1)

            def h_hi(t, i, m):
                b = unit_no(t) % 2
                act.wait_ge(ht_turned, unit_count(t, m, PER, i + 1))
                nc.scalar.activation(ht_hi[b][:, :, i * NODES:(i + 1) * NODES],
                                     ps_turn[:, 0:H].rearrange("p (c k) -> p c k", c=KT),
                                     ACT.Copy).then_inc(ht_hi_set, 1)

            def make_mask(t, m):
                b, l = unit_no(t) % 2, layer_of(t)
                act.wait_ge(adj_loaded[b], adj_count(t, m))
                nc.scalar.activation(mask[b][:, :, :], adj_u8[b][:, :, :], ACT.Identity,
                                     bias=mask_shift[l][:, :], scale=mask_scale[l][:, :]).then_inc(mask_set, 1)

            def slot(t, m):
                for i in range(PER):
                    lt, li = lag_of(t, i)
                    nt, ni = next_of(t + 2, i)
                    if exists(lt):
                        probs_hi(lt, li, m)
                    if exists(t + 2):
                        h_hi(t + 2, i, m)
                    if exists(nt):
                        relu(nt, ni, m)
                    if t == 1:
                        weights_hi(1, CAST_ORDER[i])
                    if exists(t + 1):
                        v_hi_out(t + 1, i, m)
                        for chunk in chunks_done(i, 0):
                            qk_hi_out(t + 1, chunk, m)
                    if exists(lt):
                        ctx_hi(lt, li, m)
                    if exists(t):
                        exp(t, i, m)
                    if exists(t + 1):
                        for chunk in chunks_done(i, 1) + chunks_done(i, 2):
                            qk_hi_out(t + 1, chunk, m)
                        if i == 2:
                            make_mask(t + 1, m)

            relu(0, 0, None)
            slot(FIRST, None)
            for j in CAST_ORDER:
                weights_hi(0, j)
            over_slots(act, slot)

        @block.vector
        def _(dve):
            count = dve.alloc_register("count")
            chained = [0]

            def then(instruction):
                chained[0] += 1
                instruction.then_inc(setup_chain, 1)
                dve.wait_ge(setup_chain, chained[0])

            def spread_biases(l):
                dve.wait_ge(b_loaded[l], 64)
                if l:
                    dve.wait_ge(out_bias_summed, l)
                for c in range(KT):
                    ins = nc.vector.tensor_scalar(v_bias_wide[:, c, :], ones[:, :], v_bias_raw[l][:, c:c + 1], None,
                                                  ALU.mult)
                ins.then_inc(v_bias_spread, 1)
                nc.vector.tensor_reduce(largest[:, 4:6], qk_bias_raw[l][:, :, :], AX_X, ALU.max,
                                        apply_absolute_value=True).then_inc(largest_found, 1)

            def find_largest(l, j):
                dve.wait_ge(w_loaded[l][j], 16)
                nc.vector.tensor_reduce(largest[:, j:j + 1], w_raw[l][j][:, :, :].rearrange("p c n -> p (c n)"),
                                        AX_X, ALU.max, apply_absolute_value=True).then_inc(largest_found, 1)

            def find_scales(l):
                dve.wait_ge(largest_shared, l + 1)
                then(nc.vector.tensor_scalar(bound[:, 0:3], largest_all[:, 0:3], float(H), LEAST, ALU.mult, ALU.max))
                nc.vector.tensor_scalar(bound[:, 3:4], largest_all[:, 3:4], LEAST, None, ALU.max)
                then(nc.vector.tensor_tensor(bound[:, 0:2], bound[:, 0:2], largest_all[:, 4:6], ALU.add))
                then(nc.vector.tensor_scalar(power[:, :].bitcast(I32), bound[:, :].bitcast(I32), 0x7F800000, None,
                                             ALU.bitwise_and))
                nc.vector.tensor_tensor(both[:, :], power[:, 0:4:2], power[:, 1:4:2], ALU.mult)
                then(nc.vector.reciprocal(inverse[:, :], power[:, :]))
                nc.vector.tensor_scalar(w_scale[l][:, 0:3], inverse[:, 0:3], PROJ_TOP, None, ALU.mult)
                nc.vector.tensor_scalar(w_scale[l][:, 3:4], inverse[:, 3:4], OUT_TOP, None, ALU.mult)
                nc.vector.tensor_scalar(b_scale[:, :], inverse[:, 0:2], PROJ_TOP * HS, None, ALU.mult)
                nc.vector.tensor_scalar(out_scale[l][:, :], both[:, 1:2], 1.0 / (PROJ_TOP * HS * OUT_TOP), None,
                                        ALU.mult)
                then(nc.vector.tensor_scalar(exp_scale[l][:, :], both[:, 0:1],
                                             float(DH) ** -0.5 / (PROJ_TOP * HS) ** 2, None, ALU.mult))
                then(nc.vector.reciprocal(exp_inverse[:, :], exp_scale[l][:, :]))
                nc.vector.tensor_scalar(mask_scale[l][:, :], exp_inverse[:, :], NEG, None, ALU.mult)
                nc.vector.tensor_scalar(mask_shift[l][:, :], exp_inverse[:, :], -NEG, None, ALU.mult)
                for j in range(2):
                    ins = nc.vector.tensor_scalar(qk_bias[l][:, j, :], qk_bias_raw[l][:, j, :], b_scale[:, j:j + 1],
                                                  None, ALU.mult)
                ins.then_inc(scales_set, 1)

            def weights_lo(l, j):
                dve.wait_ge(w_hi_set, 4 * l + CAST_ORDER.index(j) + 1)
                nc.vector.scalar_tensor_tensor(out=w_lo[l][j][:, :, :], in0=w_raw[l][j][:, :, :],
                                               scalar=w_scale[l][:, j:j + 1], in1=w_hi[l][j][:, :, :],
                                               op0=ALU.mult, op1=ALU.subtract).then_inc(weights_set, 1)

            def keep_out_bias(l):
                dve.wait_ge(out_bias_summed, l + 1)
                nc.vector.tensor_copy(out_bias[l][:, :], ps_pt[l][:, 0:H]).then_inc(out_bias_set, 1)

            def statistics(t, i, m):
                done = unit_count(t, m, PER, i + 1)
                g = group_of(t)
                if layer_of(t) == 0 and i == 0:
                    dve.wait_ge(x_loaded[x_buffer(g)], x_count(g, m))
                if layer_of(t) == 1:
                    dve.wait_ge(out_added, unit_count(first_layer_slot(g), m, PER, i + 1))
                xs = x_of(t)[:, i, :]
                nc.vector.bn_stats(stats[i % 2][:, :], xs).then_inc(stats_found, 1)
                wait_apart(dve, count, stats_found, done)
                nc.vector.bn_aggr(mean_var[i % 2][:, :], stats[i % 2][:, :]).then_inc(mean_found, 1)

            def probs_lo(t, i, m):
                for s in range(2):
                    dve.wait_ge(pt_hi_set, unit_count(t, m, 2 * PER, 2 * i + 1 + s))
                    nc.vector.tensor_tensor(pt_lo[:, s * PAIRS:(s + 1) * PAIRS, :],
                                            ps_pt[s][:, 0:PAIRS * P].rearrange("p (a k) -> p a k", a=PAIRS),
                                            pt_hi[:, s * PAIRS:(s + 1) * PAIRS, :], ALU.subtract
                                            ).then_inc(pt_set, 1)

            def v_lo_out(t, i, m):
                b, job = unit_no(t) % 2, job_of("v", i)
                dve.wait_ge(proj_hi_set, unit_count(t, m, JOBS, job + 1))
                nc.vector.tensor_tensor(v_lo[b][:, i, :, 0:DH],
                                        ps_proj[JOB_LIST[job][2]][:, 0:H].rearrange("p (a d) -> p a d", a=HEADS),
                                        v_hi[b][:, i, :, 0:DH], ALU.subtract).then_inc(proj_set, 1)

            def qk_lo_out(t, chunk, m):
                b, job = unit_no(t) % 2, job_of("qk", chunk)
                dve.wait_ge(proj_hi_set, unit_count(t, m, JOBS, job + 1))
                nc.vector.scalar_tensor_tensor(
                    out=qk_lo[b][:, chunk, :], in0=ps_proj[JOB_LIST[job][2]][:, :],
                    scalar=qk_bias[layer_of(t)][:, chunk // KT, chunk % KT:chunk % KT + 1],
                    in1=qk_hi[b][:, chunk, :], op0=ALU.add, op1=ALU.subtract).then_inc(proj_set, 1)

            def normalise(t, i, m):
                done = unit_count(t, m, PER, i + 1)
                dve.wait_ge(ctx_summed, done)
                summed = ps_out[:, 0:HEADS * VW].rearrange("p (a d) -> p a d", a=HEADS)
                nc.vector.reciprocal(row_rcp[:, :].rearrange("p (a o) -> p a o", o=1),
                                     summed[:, :, DH:DH + 1]).then_inc(rcp_ready, 1)
                dve.wait_ge(rcp_ready, done)
                nc.vector.tensor_tensor(ctx_n[:, :, :], summed[:, :, 0:DH],
                                        row_rcp[:, :].rearrange("p (a o) -> p a o", o=1)
                                        .to_broadcast([P, HEADS, DH]), ALU.mult).then_inc(ctx_ready, 1)

            def mask_and_max(t, i, half, m):
                b = unit_no(t) % 2
                if half == 0:
                    wait_apart(dve, count, scored, unit_count(t, m, PER, i + 1))
                for s in range(half * PAIRS, (half + 1) * PAIRS):
                    ins = nc.vector.tensor_tensor_reduce(
                        probs[:, s, :], ps_scores[s // PAIRS][:, (s % PAIRS) * P:(s % PAIRS + 1) * P],
                        mask[b][:, i, :], 1.0, -3.0e38, ALU.add, ALU.max, row_max[:, s:s + 1])
                if half == 1:
                    ins.then_inc(masked, 1)

            def subtract_max(t, i, m):
                done = unit_count(t, m, PER, i + 1)
                dve.wait_ge(masked, done)
                nc.vector.tensor_tensor(probs[:, :, :], probs[:, :, :],
                                        row_max[:, :].rearrange("p (a o) -> p a o", o=1)
                                        .to_broadcast([P, HEADS, NODES]), ALU.subtract).then_inc(shifted, 1)

            def ctx_lo(t, i, m):
                dve.wait_ge(ct_hi_set, unit_count(t, m, PER, i + 1))
                nc.vector.tensor_tensor(ct_lo[:, :, :], ps_turn[:, 0:H].rearrange("p (c k) -> p c k", c=KT),
                                        ct_hi[:, :, :], ALU.subtract).then_inc(ct_set, 1)

            def add_residual(t, i, m):
                l, g = layer_of(t), group_of(t)
                dve.wait_ge(out_summed, unit_count(t, m, PER, i + 1))
                dve.wait_ge(res_ready, unit_count(t, m, PER, i + 1))
                if l and g >= 1:
                    wait(dve, stored[i], group_count(t, m, 16))
                src, dst = x_of(t), x2 if l else x1[g % X1_BUFFERS]
                nc.vector.scalar_tensor_tensor(out=dst[:, i, :], in0=ps_out[:, 0:H], scalar=out_scale[l][:, :],
                                               in1=src[:, i, :], op0=ALU.mult, op1=ALU.add).then_inc(out_added, 1)

            def h_lo(t, i, m):
                b = unit_no(t) % 2
                dve.wait_ge(ht_hi_set, unit_count(t, m, PER, i + 1))
                rows = slice(i * NODES, (i + 1) * NODES)
                nc.vector.tensor_tensor(ht_lo[b][:, :, rows], ps_turn[:, 0:H].rearrange("p (c k) -> p c k", c=KT),
                                        ht_hi[b][:, :, rows], ALU.subtract).then_inc(ht_set, 1)

            def slot(t, m):
                for i in range(PER):
                    lt, li = lag_of(t, i)
                    nt, ni = next_of(t + 2, i)
                    if (t, i) == (FIRST, 3):
                        spread_biases(0)
                        for j in range(4):
                            find_largest(0, j)
                        find_scales(0)
                    if exists(nt):
                        statistics(nt, ni, m)
                    if exists(lt):
                        probs_lo(lt, li, m)
                    if exists(t):
                        mask_and_max(t, i, 0, m)
                        mask_and_max(t, i, 1, m)
                    if exists(t + 2):
                        h_lo(t + 2, i, m)
                    if (t, i) == (-1, 0):
                        spread_biases(1)
                    if t == -1:
                        find_largest(1, i)
                    if t == 1:
                        weights_lo(1, CAST_ORDER[i])
                    if exists(lt) and i % 2 == 0:
                        normalise(lt, li, m)
                    if exists(t + 1):
                        v_lo_out(t + 1, i, m)
                    if exists(lt) and i % 2 == 1:
                        normalise(lt, li, m)
                    if exists(t):
                        subtract_max(t, i, m)
                    if exists(lt):
                        ctx_lo(lt, li, m)
                    if exists(t + 1):
                        for chunk in chunks_done(i, 0) + chunks_done(i, 1) + chunks_done(i, 2):
                            qk_lo_out(t + 1, chunk, m)
                    if exists(lt):
                        add_residual(lt, li, m)
                    if (t, i) == (0, 2):
                        find_scales(1)
                    if (t, i) == (-1, 3):
                        keep_out_bias(1)

            dve.wait_ge(consts_set, CONSTS)
            statistics(0, 0, None)
            slot(FIRST, None)
            for j in CAST_ORDER:
                weights_lo(0, j)
            keep_out_bias(0)
            over_slots(dve, slot)


_WEIGHTS = ("Wq", "bq", "Wk", "bk", "Wv", "bv", "Wf", "bf")


def kernel(**inputs):
    import concourse.bacc as bacc
    from concourse.bass_utils import run_bass_kernel_spmd

    nc = bacc.Bacc("TRN2", target_bir_lowering=False, num_devices=1)
    arrays, aps = {}, {}
    for name, a in inputs.items():
        a = np.ascontiguousarray(a)
        arrays[f"in_{name}"] = a
        aps[name] = nc.dram_tensor(f"in_{name}", a.shape, mybir.dt.from_np(a.dtype), kind="ExternalInput").ap()
    out = nc.dram_tensor("out_x", inputs["x"].shape, F32, kind="ExternalOutput").ap()
    layers = [{w: aps[f"L{l}_gnn_{w}"] for w in _WEIGHTS} for l in range(LAYERS)]
    build(nc, aps["x"], aps["adj"], layers, out)
    r = run_bass_kernel_spmd(nc, [arrays], core_ids=[0])
    return r.results[0]["out_x"]
```
